# Optimizing a Trainium2 kernel written in Bass

```python
import numpy as np
import jax
import jax.numpy as jnp

def _softmax(x, axis=-1):
    return jax.nn.softmax(x, axis=axis)

def _gelu(x):
    return jax.nn.gelu(x, approximate=True)

def _silu(x):
    return jax.nn.silu(x)

def _sigmoid(x):
    return jax.nn.sigmoid(x)

def _layernorm(x, axis=-1, eps=1e-05):
    m = jnp.mean(x, axis=axis, keepdims=True)
    v = jnp.var(x, axis=axis, keepdims=True)
    return (x - m) / jnp.sqrt(v + eps)

def _scatter_add(tgt, idx, src, axis=0):
    return tgt.at[idx].add(src)

def _segment_sum(src, seg, n):
    return jax.ops.segment_sum(src, seg, n)
kernel_name = 'mk_seq_preln_d1_jaxref_r8_a8c573'

def setup_inputs(seed: int=0):
    np.random.seed(seed)
    _w = jnp.asarray

    def _L0_attn_setup():
        import jax, jax.numpy as jnp
        import numpy as np
        B, T, E, H = (2, 256, 128, 16)
        D = E // H
        key = jax.random.key(seed)
        k = jax.random.split(key, 6)
        return {'x': jax.random.normal(k[0], (B, T, E), dtype=jnp.float32), 'w_att_val': jax.random.normal(k[1], (H, D, D), dtype=jnp.float32) * (6.0 / D) ** 0.5, 'wv_w': jax.random.normal(k[2], (E, E), dtype=jnp.float32) * E ** (-0.5), 'wv_b': jnp.zeros((E,), dtype=jnp.float32), 'out_w': jax.random.normal(k[3], (E, E), dtype=jnp.float32) * E ** (-0.5), 'out_b': jnp.zeros((E,), dtype=jnp.float32)}
    _L0_attn_in = _L0_attn_setup()

    def _L0_ffn_setup():
        import jax, jax.numpy as jnp
        import numpy as np
        B, T, C, E, K, CAP, H = (8, 256, 128, 8, 2, 512, 512)
        key = jax.random.key(seed)
        ks = jax.random.split(key, 6)
        s = 0.02
        return {'x': jax.random.normal(ks[0], (B, T, C), jnp.float32), 'rw1': s * jax.random.normal(ks[1], (C, H), jnp.float32), 'rb1': jnp.zeros((H,), jnp.float32), 'rw2': s * jax.random.normal(ks[2], (H, E), jnp.float32), 'rb2': jnp.zeros((E,), jnp.float32), 'ew1': s * jax.random.normal(ks[3], (E, C, H), jnp.float32), 'eb1': jnp.zeros((E, H), jnp.float32), 'ew2': s * jax.random.normal(ks[4], (E, H, C), jnp.float32), 'eb2': jnp.zeros((E, C), jnp.float32)}
    _L0_ffn_in = _L0_ffn_setup()
    _d = {'L0_attn_x': _L0_attn_in['x'], 'L0_attn_w_att_val': _L0_attn_in['w_att_val'], 'L0_attn_wv_w': _L0_attn_in['wv_w'], 'L0_attn_wv_b': _L0_attn_in['wv_b'], 'L0_attn_out_w': _L0_attn_in['out_w'], 'L0_attn_out_b': _L0_attn_in['out_b'], 'L0_ffn_rw1': _L0_ffn_in['rw1'], 'L0_ffn_rb1': _L0_ffn_in['rb1'], 'L0_ffn_rw2': _L0_ffn_in['rw2'], 'L0_ffn_rb2': _L0_ffn_in['rb2'], 'L0_ffn_ew1': _L0_ffn_in['ew1'], 'L0_ffn_eb1': _L0_ffn_in['eb1'], 'L0_ffn_ew2': _L0_ffn_in['ew2'], 'L0_ffn_eb2': _L0_ffn_in['eb2']}
    _x0 = _d['L0_attn_x']
    _d['L0_attn_x'] = jax.random.normal(jax.random.fold_in(jax.random.key(seed), 1), (8, 512, 128), dtype=_x0.dtype)
    del _x0
    return _d

def reference(L0_attn_x, L0_attn_w_att_val, L0_attn_wv_w, L0_attn_wv_b, L0_attn_out_w, L0_attn_out_b, L0_ffn_rw1, L0_ffn_rb1, L0_ffn_rw2, L0_ffn_rb2, L0_ffn_ew1, L0_ffn_eb1, L0_ffn_ew2, L0_ffn_eb2):

    def _L0_attn_ref(x, w_att_val, wv_w, wv_b, out_w, out_b):
        import jax, jax.numpy as jnp
        import numpy as np
        B, T, E, H = (2, 256, 128, 16)
        D = E // H
        b, t, e = x.shape
        h, d, _ = w_att_val.shape
        x_h = x.reshape(b, t, h, d).transpose(0, 2, 1, 3)
        xw = jnp.einsum('bhtd,hde->bhte', x_h, w_att_val)
        att = jnp.einsum('bhte,bhse->bhts', xw, x_h) / jnp.sqrt(jnp.asarray(d, x.dtype))
        att = jax.nn.softmax(att, axis=-1)
        vx = x @ wv_w.T + wv_b
        vx = vx.reshape(b, t, h, d).transpose(0, 2, 1, 3)
        o = jnp.einsum('bhts,bhsd->bhtd', att, vx)
        o = o.transpose(0, 2, 1, 3).reshape(b, t, e)
        return o @ out_w.T + out_b

    def _L0_ffn_ref(x, rw1, rb1, rw2, rb2, ew1, eb1, ew2, eb2):
        import jax, jax.numpy as jnp
        import numpy as np
        B, T, C, E, K, CAP, H = (8, 256, 128, 8, 2, 512, 512)
        Bx, Tx, Cx = x.shape
        N = Bx * Tx
        logits = jax.nn.relu(x @ rw1 + rb1) @ rw2 + rb2
        vals, ids = jax.lax.top_k(logits, K)
        probs = jax.nn.softmax(vals, axis=-1)
        ids_f = ids.reshape(N * K)
        probs_f = probs.reshape(N * K)
        xr = jnp.repeat(x.reshape(N, Cx), K, axis=0)
        m = jax.nn.one_hot(ids_f, E, dtype=jnp.int32)
        pos = jnp.cumsum(m, axis=0) - 1
        pos_tok = jnp.take_along_axis(pos, ids_f[:, None], axis=1)[:, 0]
        keep = (pos_tok < CAP).astype(x.dtype)
        pos_c = jnp.clip(pos_tok, 0, CAP - 1)
        disp = jnp.zeros((E, CAP, Cx), x.dtype).at[ids_f, pos_c].add(xr * keep[:, None])
        h = jax.nn.relu(jnp.einsum('enc,ech->enh', disp, ew1) + eb1[:, None, :])
        eo = jnp.einsum('enh,ehc->enc', h, ew2) + eb2[:, None, :]
        y = eo[ids_f, pos_c] * (probs_f * keep)[:, None]
        return y.reshape(Bx, Tx, K, Cx).sum(axis=2)
    x = L0_attn_x
    x = x + _L0_attn_ref(_layernorm(x, axis=-1), L0_attn_w_att_val, L0_attn_wv_w, L0_attn_wv_b, L0_attn_out_w, L0_attn_out_b)
    x = x + _L0_ffn_ref(_layernorm(x, axis=-1), L0_ffn_rw1, L0_ffn_rb1, L0_ffn_rw2, L0_ffn_rb2, L0_ffn_ew1, L0_ffn_eb1, L0_ffn_ew2, L0_ffn_eb2)
    return x

_drawn_inputs = setup_inputs


def setup_inputs(seed=0):
    import zlib

    import numpy as np

    out = dict(_drawn_inputs(seed))
    spreads = {'L0_attn_wv_b': (0.0, 0.1),
     'L0_attn_out_b': (0.0, 0.1),
     'L0_ffn_rb1': (0.0, 0.1),
     'L0_ffn_rb2': (0.0, 0.1),
     'L0_ffn_eb1': (0.0, 0.757),
     'L0_ffn_eb2': (0.0, 0.1)}
    factors = {'L0_ffn_ew1': 2.693}
    for name, (base, spread) in spreads.items():
        noise = np.random.default_rng([zlib.crc32(name.encode()), seed]).standard_normal(out[name].shape)
        drawn = base * np.exp(spread * noise) if base else spread * noise
        out[name] = jnp.asarray(drawn.astype(out[name].dtype))
    for name, factor in factors.items():
        out[name] = (out[name] * factor).astype(out[name].dtype)
    return out
```

```python
from contextlib import ExitStack

import concourse.bass as bass
from concourse import mybir

F32 = mybir.dt.float32
BF16 = mybir.dt.bfloat16
I32 = mybir.dt.int32
U32 = mybir.dt.uint32
ALU = mybir.AluOpType
ACT = mybir.ActivationFunctionType
AXIS = mybir.AxisListType

P = 128
NB, T, C = 8, 512, 128
NH, D = 16, 8
TT = T // P
HG = 4
GB = NH // HG
NG = NB * GB
STACK = 64
PARTS = 6
MROW = PARTS * D
NE, CAP, HID = 8, 512, 512
HC = HID // P
NTOK = NB * T
REC = C + 2
SCALE = float(D) ** -0.5
EPS = 1e-5
DROPPED = float(1 << 20)
SLOTS = 8

SHARED = [
    (0, 1, "kT", 2, 0, 0), (0, 2, "qT", 2, 0, 0), (0, 3, "avT", -1, 0, 0),
    (0, 4, "oT", -1, 1, 0), (0, 5, "zT", 1, 1, 0), (0, 6, "mT", 1, 0, 0), (0, 7, "qv", 1, 2, 0),
    (1, 0, "out", -1, 1, 0), (1, 1, "kT", 2, 0, 0), (1, 2, "qT", 2, 0, 0), (1, 3, "avT", -1, 0, 0),
    (1, 4, "qv", 1, 2, 1), (1, 6, "mT", 1, 0, 0), (1, 7, "yT", -1, 1, 0),
    (2, 0, "hid", -1, 4, 0), (2, 1, "kT", 2, 0, 0), (2, 2, "qT", 2, 0, 0), (2, 3, "avT", -1, 0, 0),
    (2, 4, "hid", -1, 4, 1), (2, 5, "hid", -1, 4, 2), (2, 6, "mT", 1, 0, 0), (2, 7, "hid", -1, 4, 3),
    (3, 0, "logit", -1, 1, 0), (3, 1, "kT", 2, 0, 0), (3, 2, "qT", 2, 0, 0), (3, 3, "avT", -1, 0, 0),
    (3, 4, "rank", -1, 1, 0), (3, 6, "mT", 1, 0, 0),
]
USES = ("kT", "qT", "mT", "avT", "oT", "zT", "qv", "out", "yT", "hid", "logit", "rank")


def live(i, n):
    return not isinstance(i, int) or 0 <= i < n


def need(eng, sem, count):
    if not isinstance(count, int) or count > 0:
        eng.wait_ge(sem, count)


def use_index(b, use):
    g, _, _, off, per, _ = use
    return b + off if per else GB * b + g + off


def use_exists(b, use):
    return live(use_index(b, use), NB if use[4] else NG)


def use_count(b, use):
    i = use_index(b, use)
    return i * use[4] + use[5] + 1 if use[4] else i + 1


def use_before(b, k):
    for back in range(4):
        for n in reversed(range(k if back == 0 else len(SHARED))):
            if use_exists(b - back, SHARED[n]):
                return SHARED[n][2], use_count(b - back, SHARED[n])
    return None


def half(i):
    return i // 2


def run_batches(eng, body):
    body(-1)
    body(0)
    body(1)
    with eng.Fori(2, NB - 1) as b:
        body(b)
    body(NB - 1)
    body(NB)


def build(nc, x, w_att, wv_w, wv_b, out_w, out_b, rw1, rb1, rw2, rb2, ew1, eb1, ew2, eb2, out):
    x2_d = nc.dram_tensor("x2_scratch", (NTOK, C), F32).ap()
    rec_d = nc.dram_tensor("dispatched_rows", (NE * CAP, REC), F32).ap()
    y_d = nc.dram_tensor("expert_rows", (2 * NTOK, C), F32).ap()
    x_in = x.rearrange("b (p t) c -> b p t c", t=TT)
    x2_v = x2_d.rearrange("(b p t) c -> b p t c", p=P, t=TT)
    rec_v = rec_d.rearrange("(e p n) r -> e p n r", p=P, n=TT)
    y_v = y_d.rearrange("(k b p t) c -> k b p t c", k=2, p=P, t=TT)
    out_v = out.rearrange("b (p t) c -> b p t c", t=TT)

    with ExitStack() as ctx:
        def sb(name, shape, dt=F32):
            return ctx.enter_context(nc.sbuf_tensor(name, shape, dt))

        def sem(name):
            return ctx.enter_context(nc.semaphore(name))

        ident = sb("ident", [P, P])
        identb = sb("identb", [P, P], BF16)
        before = sb("before", [P, P], BF16)
        onesb = sb("onesb", [P, P], BF16)
        ones1 = sb("ones1", [1, P])
        w_small = sb("w_small", [P, D])
        w_qv = sb("w_qv", [P, 2, C])
        w_raw = sb("w_raw", [P, 2, C])
        w_out = sb("w_out", [P, C])
        bv_row = sb("bv_row", [P, C])
        bo_row = sb("bo_row", [P, C])
        b_raw = sb("b_raw", [NE * HC + HC, P])
        b_hid = sb("b_hid", [P, NE * HC + HC])
        rw1_s = sb("rw1_s", [P, HID])
        rw2_s = sb("rw2_s", [P, HC, NE])
        rb2_row = sb("rb2_row", [P, NE])
        neg_half = sb("neg_half", [P, TT])
        falling = sb("falling", [P, 1, NE])
        slot_base = sb("slot_base", [P, 1, NE])
        x_a = sb("x_a", [P, TT, C])
        x_b = sb("x_b", [P, TT, C])
        x_bo = sb("x_bo", [P, TT, C])
        stat_a = sb("stat_a", [P, TT, 6])
        mv_a = sb("mv_a", [P, TT, 2])
        ln_a = sb("ln_a", [P, 3, TT])
        z = sb("z", [P, TT, C])
        zT = sb("zT", [P, T])
        qv = sb("qv", [P, TT, 2, C])
        stage = sb("stage", [P, 2, TT, HG, D], BF16)
        rest = sb("rest", [P, 2, TT, HG, D])
        qa = [sb(f"qa{i}", [P, TT, HG, STACK], BF16) for i in range(4)]
        ka = [sb(f"ka{i}", [P, TT, HG, STACK], BF16) for i in range(4)]
        va = [sb(f"va{i}", [P, TT, HG, 32]) for i in range(4)]
        ks = [sb(f"ks{i}", [P, HG, T], BF16) for i in range(4)]
        qs = [sb(f"qs{i}", [P, 2, T], BF16) for i in range(2)]
        qm = [sb(f"qm{i}", [P, 2, T], BF16) for i in range(2)]
        neg_max = [sb(f"neg_max{i}", [P, TT, HG, 1]) for i in range(2)]
        probs = sb("probs", [P, TT, HG, T])
        av = sb("av", [P, T])
        inv_sum = sb("inv_sum", [P, TT, HG, 1])
        o_tok = sb("o_tok", [P, TT, NH, D])
        oT = sb("oT", [P, T])
        x2 = sb("x2", [P, TT, C])
        stat_b = sb("stat_b", [P, TT, 6])
        mv_b = sb("mv_b", [P, TT, 2])
        ln_b = sb("ln_b", [P, 3, TT])
        rec = sb("rec", [P, TT, 2, REC])
        yT = sb("yT", [P, T])
        hid = sb("hid", [P, HC, T])
        logits = sb("logits", [P, TT, NE])
        tmp = sb("tmp", [P, TT, NE])
        top = sb("top", [P, 2, TT, 1])
        pick = sb("pick", [P, 2, TT, 1])
        chosen = sb("chosen", [P, 2, TT, NE])
        mask = sb("mask", [P, TT, NE], BF16)
        gap = sb("gap", [P, TT])
        e_gap = sb("e_gap", [P, TT])
        den = sb("den", [P, TT])
        taken = sb("taken", [P, NE])
        pos = sb("pos", [P, TT, NE])
        over = sb("over", [P, TT, NE])
        addr = sb("addr", [P, 1, TT, NE])
        slot_e = sb("slot_e", [P, 2, TT, NE])
        slot_f = sb("slot_f", [P, 2, TT, 1])
        slot = sb("slot", [P, 2, TT, 1], I32)
        dest = sb("dest", [P, TT, 2])
        blank = sb("blank", [P, NE * TT, REC])
        rec_l = [sb(f"rec_l{i}", [P, TT, REC]) for i in range(2)]
        w1 = [sb(f"w1_{i}", [P, HID]) for i in range(2)]
        w2 = [sb(f"w2_{i}", [P, HC, C]) for i in range(2)]
        b2 = [sb(f"b2_{i}", [1, C]) for i in range(2)]
        xT = [sb(f"xT{i}", [P, CAP]) for i in range(2)]
        hT = [sb(f"hT{i}", [P, HC, CAP]) for i in range(2)]
        y = [sb(f"y{i}", [P, TT, C]) for i in range(2)]
        f_x = [sb(f"f_x{i}", [P, TT, C]) for i in range(2)]
        f_y = [sb(f"f_y{i}", [P, 2, TT, C]) for i in range(2)]
        f_s = [sb(f"f_s{i}", [P, TT, C]) for i in range(2)]
        f_o = [sb(f"f_o{i}", [P, TT, C]) for i in range(2)]

        ps = ctx.enter_context(nc.psum_tensor("ps", [P, 8, 512], F32))
        score = [ps[:, 0:2, :], ps[:, 2:4, :]]
        plain = [ps[:, 4, :], ps[:, 5, :]]
        acc = ps[:, 6, :]
        shared = ps[:, 7, :]
        shared_b = shared.bitcast(BF16)

        loaded = sem("loaded")
        xa_in, xb_in, x2_out = sem("xa_in"), sem("xb_in"), sem("x2_out")
        blank_out, rec_out = sem("blank_out"), sem("rec_out")
        pool_c, dve_c, act_c, pe_c = sem("pool_c"), sem("dve_c"), sem("act_c"), sem("pe_c")
        pool_waits, dve_waits = sem("pool_waits"), sem("dve_waits")
        kT_done_2 = sem("kT_done_2")
        full = {n: sem(f"{n}_full") for n in USES}
        done = {n: sem(f"{n}_done") for n in USES}
        score_full, exp_done = sem("score_full"), sem("exp_done")
        plain_full, max_done = sem("plain_full"), sem("max_done")
        av_part, av_out = sem("av_part"), sem("av_out")
        split_done, v_done, m_done = sem("split_done"), sem("v_done"), sem("m_done")
        stat_a_done, z_done = sem("stat_a_done"), sem("z_done")
        xbo_done, stat_b_done, y_norm = sem("xbo_done"), sem("stat_b_done"), sem("y_norm")
        gap_done, egap_done, mask_done, route_done = (sem("gap_done"), sem("egap_done"), sem("mask_done"),
                                                      sem("route_done"))
        split_q, split_m, ln_q, ln2_q, dest_q = (sem("split_q"), sem("split_m"), sem("ln_q"), sem("ln2_q"),
                                                 sem("dest_q"))
        st_q, st2_q, inv_q, route_q = sem("st_q"), sem("st2_q"), sem("inv_q"), sem("route_q")
        def two(name):
            return [sem(f"{name}{r}") for r in range(2)]

        w_in, rl_in, y_out = two("w_in"), two("rl_in"), two("y_out")
        xT_full, xT_done = sem("xT_full"), sem("xT_done")
        h_full, h_act, h_dve = sem("h_full"), sem("h_act"), sem("h_dve")
        y_full, y_done = sem("y_full"), sem("y_done")
        f_in, done_out = two("f_in"), two("done_out")
        f_sum, f_done = sem("f_sum"), sem("f_done")

        block = ctx.enter_context(nc.Block())

        @block.sync
        def _(sp):
            def load(dst, src):
                sp.dma_start(dst, src).then_inc(loaded, 16)

            sp.dma_start(x_a[:, :, :], x_in[0]).then_inc(xa_in, 16)
            load(w_small[:, :], w_att.rearrange("h d e -> (h d) e"))
            load(w_raw[:, 0, :], wv_w)
            load(w_raw[:, 1, :], out_w)
            load(b_raw[0:NE * HC, :], eb1.rearrange("e (c p) -> (e c) p", p=P))
            load(b_raw[NE * HC:NE * HC + HC, :], rb1.rearrange("(c p) -> c p", p=P))
            load(bv_row[:, :], wv_b.rearrange("(a c) -> a c", a=1).broadcast_to([P, C]))
            load(bo_row[:, :], out_b.rearrange("(a c) -> a c", a=1).broadcast_to([P, C]))
            load(rb2_row[:, :], rb2.rearrange("(a c) -> a c", a=1).broadcast_to([P, NE]))
            load(rw1_s[:, :], rw1)
            load(rw2_s[:, :, :], rw2.rearrange("(c p) e -> p c e", p=P))
            sp.wait_ge(pool_c, 1)
            sp.dma_start(rec_d.rearrange("(p n) r -> p n r", p=P), blank[:, :, :]).then_inc(blank_out, 16)
            for k in range(2):
                for b in range(NB):
                    sp.dma_start(y_v[k, b], blank[:, 0:TT, 0:C]).then_inc(blank_out, 16)

            def batch(b):
                f, k = b + 1, b - 1
                if live(f, NB):
                    if not isinstance(f, int) or f > 0:
                        need(sp, z_done, f)
                        sp.dma_start(x_a[:, :, :], x_in[f]).then_inc(xa_in, 16)
                if live(k, NB):
                    need(sp, xbo_done, k)
                    sp.dma_start(x_b[:, :, :], x_in[k]).then_inc(xb_in, 16)
                    sp.wait_ge(done["out"], k + 1)
                    sp.dma_start(x2_v[k], x2[:, :, :]).then_inc(x2_out, 16)

            run_batches(sp, batch)

            def expert(e, r):
                need(sp, y_out[r], 16 * TT * (half(e)))
                sp.dma_start(rec_l[r][:, :, :], rec_v[e]).then_inc(rl_in[r], 16)
                need(sp, h_full, HC * (e - 1))
                sp.dma_start(w1[r][:, :], ew1[e]).then_inc(w_in[r], 16)
                need(sp, y_full, e - 1)
                sp.dma_start(w2[r][:, :, :], ew2[e].rearrange("(c p) n -> p c n", p=P)).then_inc(w_in[r], 16)
                sp.dma_start(b2[r][:, :], eb2[bass.ds(e, 1), :]).then_inc(w_in[r], 16)

            sp.wait_ge(rec_out, 16 * 2 * TT * NB)
            expert(0, 0)
            expert(1, 1)
            with sp.Fori(1, NE // 2) as i:
                expert(2 * i, 0)
                expert(2 * i + 1, 1)

            def finish(c, r):
                need(sp, f_sum, c - 1)
                need(sp, f_done, c - 1)
                sp.dma_start(f_x[r][:, :, :], x2_v[c]).then_inc(f_in[r], 16)
                sp.dma_start(f_y[r][:, 0, :, :], y_v[0, c]).then_inc(f_in[r], 16)
                sp.dma_start(f_y[r][:, 1, :, :], y_v[1, c]).then_inc(f_in[r], 16)

            sp.wait_ge(x2_out, 16 * NB)
            for r in range(2):
                sp.wait_ge(y_out[r], 16 * TT * NE // 2)
            finish(0, 0)
            finish(1, 1)
            with sp.Fori(1, NB // 2) as i:
                finish(2 * i, 0)
                finish(2 * i + 1, 1)
            for r in range(2):
                sp.wait_ge(done_out[r], 16 * NB // 2)

        @block.tensor
        def _(pe):
            pe.wait_ge(loaded, 16 * 10)
            pe.wait_ge(pool_c, 2)
            pe.transpose(ps[:, 0, 0:P], w_raw[:, 0, :], ident[:, :])
            pe.transpose(ps[:, 0, P:2 * P], w_raw[:, 1, :], ident[:, :])
            pe.transpose(ps[:, 0, 2 * P:2 * P + NE * HC + HC], b_raw[:, :],
                         ident[0:NE * HC + HC, 0:NE * HC + HC]).then_inc(pe_c, 1)
            pe.wait_ge(act_c, 1)
            pe.wait_ge(pool_c, 3)

            def scores(G, g, j):
                st, pair = j // 2, j % 2
                if j == 0:
                    need(pe, done["mT"], G + 1)
                need(pe, exp_done, SLOTS * G + j - 1)
                for i in range(2):
                    mm = pe.matmul(score[j % 2][:, i, :], ks[g][:, 2 * pair + i, st * P:(st + 1) * P],
                                   qm[g % 2][:, pair, :], start=True, stop=True)
                mm.then_inc(score_full, 1)

            def values(G, g, st):
                if st == 0:
                    need(pe, av_out, G)
                    need(pe, v_done, G + 1)
                need(pe, exp_done, SLOTS * G + 2 * st + 2)
                for h in range(HG):
                    mm = pe.matmul(acc[32 * h:32 * h + 32, :], va[g][:, st, h, :], probs[:, st, h, :],
                                   start=(st == 0), stop=(st == TT - 1))
                mm.then_inc(av_part, 1)

            def plain_scores(X, gx, u):
                tt, h = u // HG, u % HG
                if u == 0:
                    need(pe, done["kT"], X + 1)
                    need(pe, kT_done_2, X + 1)
                    need(pe, done["qT"], X + 1)
                need(pe, max_done, TT * HG * X + u - 1)
                pe.matmul(plain[u % 2], qs[gx % 2][:, h // 2, tt * P:(tt + 1) * P],
                          ks[gx % 4][:, h, :], start=True, stop=True).then_inc(plain_full, 1)

            def stack_transposes(src):
                for pair in range(2):
                    for tt in range(TT):
                        n = pair * TT + tt
                        mm = pe.transpose(shared_b[:, n * P:(n + 1) * P],
                                          src[:, tt, 2 * pair:2 * pair + 2, :].rearrange("p h c -> p (h c)"),
                                          identb[:, :])
                return mm

            def token_transposes(tile):
                for tt in range(TT):
                    mm = pe.transpose(shared[:, tt * P:(tt + 1) * P], tile(tt), ident[:, :])
                return mm

            def shared_use(b, k):
                g, _, name, off, _, o = SHARED[k]
                i = use_index(b, SHARED[k])
                prior = use_before(b, k)
                if prior:
                    need(pe, done[prior[0]], prior[1])
                    if prior[0] == "kT":
                        need(pe, kT_done_2, prior[1])
                if name == "kT":
                    need(pe, split_done, i + 1)
                    mm = stack_transposes(ka[(g + off) % 4])
                elif name == "qT":
                    mm = stack_transposes(qa[(g + off) % 4])
                elif name == "mT":
                    need(pe, m_done, i + 1)
                    mm = stack_transposes(qa[(g + off) % 4])
                elif name == "avT":
                    need(pe, av_out, i + 1)
                    mm = token_transposes(lambda tt: av[:, tt * P:(tt + 1) * P])
                elif name == "oT":
                    need(pe, done["avT"], GB * (i + 1))
                    mm = token_transposes(lambda tt: o_tok[:, tt, :, :].rearrange("p h d -> p (h d)"))
                elif name == "zT":
                    need(pe, z_done, i + 1)
                    mm = token_transposes(lambda tt: z[:, tt, :])
                elif name == "yT":
                    need(pe, y_norm, i + 1)
                    mm = token_transposes(lambda tt: rec[:, tt, 0, 0:C])
                elif name == "qv":
                    need(pe, done["zT"], i + 1)
                    for n in range(2):
                        tt = 2 * o + n
                        mm = pe.matmul(shared[:, n * 2 * C:(n + 1) * 2 * C], zT[:, tt * P:(tt + 1) * P],
                                       w_qv[:, :, :].rearrange("p a c -> p (a c)"), start=True, stop=True)
                elif name == "out":
                    need(pe, done["oT"], i + 1)
                    for tt in range(TT):
                        mm = pe.matmul(shared[:, tt * C:(tt + 1) * C], oT[:, tt * P:(tt + 1) * P], w_out[:, :],
                                       start=True, stop=True)
                elif name == "hid":
                    need(pe, done["yT"], i + 1)
                    mm = pe.matmul(shared, rw1_s[:, o * P:(o + 1) * P], yT[:, :], start=True, stop=True)
                elif name == "logit":
                    need(pe, done["hid"], HC * (i + 1))
                    for tt in range(TT):
                        for c in range(HC):
                            mm = pe.matmul(shared[:, tt * NE:(tt + 1) * NE], hid[:, c, tt * P:(tt + 1) * P],
                                           rw2_s[:, c, :], start=(c == 0), stop=(c == HC - 1))
                elif name == "rank":
                    need(pe, mask_done, i + 1)
                    for n, w in enumerate((before, onesb)):
                        for tt in range(TT):
                            mm = pe.matmul(shared[:, n * NE:(n + 1) * NE], w[:, :], mask[:, tt, :],
                                           start=(tt == 0), stop=(tt == TT - 1))
                mm.then_inc(full[name], 1)

            def batch(b):
                for g in range(GB):
                    G = GB * b + g
                    for j in range(SLOTS):
                        if live(G, NG):
                            scores(G, g, j)
                        X, gx = (G + 1, g + 1) if j < 4 else (G + 2, g + 2)
                        if live(X, NG):
                            for u in range(2):
                                plain_scores(X, gx, (2 * j + 8) % 16 + u)
                        if j == 1 and live(G - 1, NG):
                            values(G - 1, (g - 1) % 4, 3)
                        if j >= 3 and j % 2 and live(G, NG):
                            values(G, g, (j - 3) // 2)
                        for k, use in enumerate(SHARED):
                            if use[0:2] == (g, j) and use_exists(b, use):
                                shared_use(b, k)

            run_batches(pe, batch)

            def rows_T(e, r):
                pe.wait_ge(rl_in[r], 16 * (half(e) + 1))
                need(pe, xT_done, e - 1)
                for n in range(TT):
                    mm = pe.transpose(ps[:, r, n * P:(n + 1) * P], rec_l[r][:, n, 0:C], ident[:, :])
                mm.then_inc(xT_full, 1)

            def first(e, r):
                pe.wait_ge(w_in[r], 48 * (half(e) + 1))
                pe.wait_ge(xT_done, e + 1)
                for c in range(HC):
                    need(pe, h_act if c < 2 else h_dve, 2 * (e - 1) + c % 2 + 1)
                    pe.matmul(ps[:, 2 + c, :], w1[r][:, c * P:(c + 1) * P], xT[r][:, :],
                              start=True, stop=True).then_inc(h_full, 1)

            def second(e, r):
                pe.wait_ge(h_act, 2 * (e + 1))
                pe.wait_ge(h_dve, 2 * (e + 1))
                need(pe, y_done, e - 1)
                for n in range(TT):
                    o = ps[:, 6 + r, n * C:(n + 1) * C]
                    for c in range(HC):
                        pe.matmul(o, hT[r][:, c, n * P:(n + 1) * P], w2[r][:, c, :], start=(c == 0), stop=False)
                    mm = pe.matmul(o, ones1[:, :], b2[r][:, :], start=False, stop=True)
                mm.then_inc(y_full, 1)

            pe.wait_ge(exp_done, SLOTS * NG)
            pe.wait_ge(max_done, TT * HG * NG)
            pe.wait_ge(av_out, NG)
            pe.wait_ge(done["rank"], NB)
            rows_T(0, 0)
            first(0, 0)
            rows_T(1, 1)
            second(0, 0)
            first(1, 1)
            with pe.Fori(1, NE // 2) as i:
                for r in range(2):
                    rows_T(2 * i + r, r)
                    second(2 * i + r - 1, 1 - r)
                    first(2 * i + r, r)
            second(NE - 1, 1)

        @block.scalar
        def _(act):
            act.wait_ge(pe_c, 1)
            act.activation(w_qv[:, 1, :], ps[:, 0, 0:P], ACT.Copy)
            act.activation(w_out[:, :], ps[:, 0, P:2 * P], ACT.Copy)
            act.activation(b_hid[:, :], ps[:, 0, 2 * P:2 * P + NE * HC + HC], ACT.Copy).then_inc(act_c, 1)
            act.wait_ge(act_c, 1)

            def exps(G, j):
                st, pair = j // 2, j % 2
                act.wait_ge(score_full, SLOTS * G + j + 1)
                need(act, av_part, TT * (G - 1) + st + 1)
                act.activation(probs[:, st, 2 * pair:2 * pair + 2, :], score[j % 2], ACT.Exp,
                               scale=SCALE).then_inc(exp_done, 1)

            def read_out(b, use):
                g, _, name, off, _, o = use
                i = use_index(b, use)
                dst, src, func, bias = None, shared, ACT.Copy, 0.0
                if name == "kT":
                    dst = ks[(g + off) % 4][0:STACK, 0:HG:2, :]
                    src = shared_b[0:STACK, :].rearrange("p (a t) -> p a t", a=2)
                    need(act, score_full, SLOTS * (i - 3))
                elif name == "qT":
                    dst, src = qs[(g + off) % 2][:, :, :].rearrange("p a t -> p (a t)"), shared_b
                    need(act, plain_full, TT * HG * (i - 1))
                elif name == "oT":
                    dst = oT[:, :]
                    need(act, full["out"], i)
                elif name == "zT":
                    dst = zT[:, :]
                    need(act, full["qv"], 2 * i)
                elif name == "yT":
                    dst = yT[:, :]
                    need(act, full["hid"], HC * i)
                elif name == "qv":
                    dst = qv[:, 2 * o:2 * o + 2, :, :].rearrange("p t a c -> p (t a c)")
                    need(act, split_done, GB * i)
                    need(act, v_done, GB * i)
                elif name == "hid":
                    dst, func, bias = hid[:, o, :], ACT.Relu, b_hid[:, NE * HC + o:NE * HC + o + 1]
                    need(act, full["logit"], i)
                else:
                    return
                act.wait_ge(full[name], use_count(b, use))
                act.activation(dst, src, func, bias=bias).then_inc(done[name], 1)

            def batch(b):
                for g in range(GB):
                    G = GB * b + g
                    for j in range(SLOTS):
                        if live(G, NG):
                            exps(G, j)
                        if j == 1 and live(G - 1, NG):
                            act.wait_ge(av_part, TT * G)
                            need(act, full["avT"], G - 1)
                            act.activation(av[:, :], acc, ACT.Copy).then_inc(av_out, 1)
                        for use in SHARED:
                            if use[0:2] == (g, j) and use_exists(b, use):
                                read_out(b, use)
                        if (g, j) == (3, 2) and live(b - 1, NB):
                            act.wait_ge(gap_done, b)
                            act.activation(e_gap[:, :], gap[:, :], ACT.Exp).then_inc(egap_done, 1)

            run_batches(act, batch)

            def expert(e, r):
                act.wait_ge(xT_full, e + 1)
                act.activation(xT[r][:, :], ps[:, r, :], ACT.Copy).then_inc(xT_done, 1)
                need(act, y_full, e - 1)
                for c in range(2):
                    act.wait_ge(h_full, HC * e + c + 1)
                    act.activation(hT[r][:, c, :], ps[:, 2 + c, :], ACT.Relu,
                                   bias=b_hid[:, bass.ds(HC * e + c, 1)]).then_inc(h_act, 1)

            expert(0, 0)
            expert(1, 1)
            with act.Fori(1, NE // 2) as i:
                expert(2 * i, 0)
                expert(2 * i + 1, 1)

            def store(c, r):
                act.wait_ge(f_done, c + 1)
                act.dma_start(out_v[c], f_o[r][:, :, :]).then_inc(done_out[r], 16)

            with act.Fori(0, NB // 2) as i:
                store(2 * i, 0)
                store(2 * i + 1, 1)

        @block.vector
        def _(v):
            v.memset(taken[:, :], 0.0).then_inc(dve_c, 1)
            v.wait_ge(dve_c, 1)
            v.wait_ge(loaded, 16 * 10)
            v.wait_ge(pool_c, 3)

            def statistics(src, stat, mv, q, i, ready):
                for tt in range(TT):
                    v.bn_stats(stat[:, tt, :], src[:, tt, :]).then_inc(q, 1)
                for tt in range(TT):
                    v.wait_ge(q, TT * i + tt + 1)
                    if not isinstance(i, int):
                        v.sem_inc(dve_waits, 1)
                    a = v.bn_aggr(mv[:, tt, :], stat[:, tt, :])
                a.then_inc(ready, 1)

            def read_out(b, use):
                g, _, name, off, _, o = use
                i = use_index(b, use)
                if name == "kT":
                    need(v, score_full, SLOTS * (i - 3))
                    v.wait_ge(full["kT"], i + 1)
                    v.tensor_copy(ks[(g + off) % 4][STACK:P, 1:HG:2, :],
                                  shared_b[STACK:P, :].rearrange("p (a t) -> p a t", a=2)).then_inc(kT_done_2, 1)
                elif name == "mT":
                    need(v, score_full, SLOTS * (i - 1))
                    v.wait_ge(full["mT"], i + 1)
                    v.tensor_copy(qm[(g + off) % 2][:, :, :].rearrange("p a t -> p (a t)"), shared_b)\
                     .then_inc(done["mT"], 1)
                elif name == "avT":
                    t4 = shared.rearrange("p (t h c) -> p t h c", t=TT, h=HG)
                    v.wait_ge(full["avT"], i + 1)
                    v.reciprocal(inv_sum[:, :, :, :], t4[:, :, :, D:D + 1]).then_inc(inv_q, 1)
                    v.wait_ge(inv_q, i + 1)
                    if (g + off) % GB == 0:
                        need(v, full["oT"], b + (g + off) // GB)
                    h0 = HG * ((g + off) % GB)
                    v.tensor_tensor(o_tok[:, :, h0:h0 + HG, :], t4[:, :, :, 0:D],
                                    inv_sum[:, :, :, :].broadcast_to([P, TT, HG, D]), ALU.mult)\
                     .then_inc(done["avT"], 1)
                elif name == "out":
                    v.wait_ge(xbo_done, i + 1)
                    need(v, x2_out, 16 * i)
                    need(v, y_norm, i)
                    v.wait_ge(full["out"], i + 1)
                    v.tensor_tensor(x2[:, :, :].rearrange("p t c -> p (t c)"), shared,
                                    x_bo[:, :, :].rearrange("p t c -> p (t c)"), ALU.add)\
                     .then_inc(done["out"], 1)
                    v.wait_ge(done["out"], i + 1)
                    statistics(x2, stat_b, mv_b, st2_q, i, stat_b_done)
                elif name == "logit":
                    choose(i)
                elif name == "rank":
                    place(i)

            NCHOOSE, NPLACE = 11, 14

            def choose(i):
                base, n = (NCHOOSE + NPLACE) * i, 0

                def step(ins):
                    nonlocal n
                    n += 1
                    ins.then_inc(route_q, 1)
                    v.wait_ge(route_q, base + n)

                v.wait_ge(full["logit"], i + 1)
                need(v, egap_done, i)
                v.tensor_tensor(logits[:, :, :], shared[:, 0:TT * NE].rearrange("p (t e) -> p t e", t=TT),
                                rb2_row[:, :].rearrange("p (a e) -> p a e", a=1).broadcast_to([P, TT, NE]),
                                ALU.add).then_inc(done["logit"], 1)
                v.wait_ge(done["logit"], i + 1)
                for k in range(2):
                    step(v.tensor_reduce(top[:, k, :, :], logits[:, :, :], AXIS.X, ALU.max))
                    step(v.tensor_tensor(tmp[:, :, :], logits[:, :, :], top[:, k, :, :].broadcast_to([P, TT, NE]),
                                         ALU.is_equal))
                    step(v.tensor_tensor(tmp[:, :, :], tmp[:, :, :], falling[:, :, :].broadcast_to([P, TT, NE]),
                                         ALU.mult))
                    step(v.tensor_reduce(pick[:, k, :, :], tmp[:, :, :], AXIS.X, ALU.max))
                    step(v.tensor_tensor(chosen[:, k, :, :], falling[:, :, :].broadcast_to([P, TT, NE]),
                                         pick[:, k, :, :].broadcast_to([P, TT, NE]), ALU.is_equal))
                    if k == 0:
                        step(v.scalar_tensor_tensor(out=logits[:, :, :], in0=chosen[:, 0, :, :], scalar=-3.0e38,
                                                    in1=logits[:, :, :], op0=ALU.mult, op1=ALU.add))
                v.tensor_tensor(gap[:, :], top[:, 1, :, 0], top[:, 0, :, 0], ALU.subtract).then_inc(gap_done, 1)
                need(v, full["rank"], i)
                v.tensor_tensor(mask[:, :, :], chosen[:, 0, :, :], chosen[:, 1, :, :], ALU.add)\
                 .then_inc(mask_done, 1)
                assert n == NCHOOSE

            def place(i):
                base, n = (NCHOOSE + NPLACE) * i + NCHOOSE, 0

                def step(ins):
                    nonlocal n
                    n += 1
                    ins.then_inc(route_q, 1)
                    v.wait_ge(route_q, base + n)

                v.wait_ge(egap_done, i + 1)
                step(v.tensor_scalar(den[:, :], e_gap[:, :], 1.0, None, ALU.add))
                need(v, rec_out, 16 * 2 * TT * i)
                step(v.reciprocal(den[:, :], den[:, :]))
                step(v.tensor_copy(rec[:, :, 0, C], den[:, :]))
                step(v.tensor_tensor(rec[:, :, 1, C], e_gap[:, :], den[:, :], ALU.mult))
                v.wait_ge(full["rank"], i + 1)
                step(v.tensor_tensor(pos[:, 0, :], shared[:, 0:NE], taken[:, :], ALU.add))
                v.tensor_tensor(taken[:, :], shared[:, NE:2 * NE], taken[:, :], ALU.add).then_inc(done["rank"], 1)
                for tt in range(1, TT):
                    step(v.tensor_tensor(pos[:, tt, :], pos[:, tt - 1, :], mask[:, tt - 1, :], ALU.add))
                step(v.tensor_scalar(over[:, :, :], pos[:, :, :], float(CAP), DROPPED, ALU.is_ge, ALU.mult))
                step(v.tensor_tensor(over[:, :, :], over[:, :, :], pos[:, :, :], ALU.add))
                step(v.tensor_tensor(addr[:, 0, :, :], over[:, :, :], slot_base[:, :, :].broadcast_to([P, TT, NE]),
                                     ALU.add))
                for k in range(2):
                    step(v.tensor_tensor(slot_e[:, k, :, :], chosen[:, k, :, :], addr[:, 0, :, :], ALU.mult))
                need(v, rec_out, 16 * 2 * TT * i)
                step(v.tensor_reduce(slot_f[:, :, :, :], slot_e[:, :, :, :], AXIS.X, ALU.add))
                v.tensor_copy(slot[:, :, :, :], slot_f[:, :, :, :]).then_inc(route_done, 1)
                v.wait_ge(done["rank"], i + 1)
                assert n == NPLACE

            def batch(b):
                for g in range(GB):
                    G = GB * b + g
                    for j in range(SLOTS):
                        X, gx = (G + 1, g + 1) if j < 4 else (G + 2, g + 2)
                        if live(X, NG):
                            for u in range((2 * j + 8) % 16, (2 * j + 8) % 16 + 2):
                                if u == 0:
                                    need(v, m_done, X - 1)
                                v.wait_ge(plain_full, TT * HG * X + u + 1)
                                v.tensor_reduce(neg_max[gx % 2][:, u // HG, u % HG, :], plain[u % 2], AXIS.X,
                                                ALU.max, negate=True).then_inc(max_done, 1)
                        if (g, j) == (0, 0) and live(b + 1, NB):
                            v.wait_ge(xa_in, 16 * (b + 2))
                            need(v, z_done, b + 1)
                            statistics(x_a, stat_a, mv_a, st_q, b + 1, stat_a_done)
                        for use in SHARED:
                            if use[0:2] == (g, j) and use_exists(b, use):
                                read_out(b, use)

            run_batches(v, batch)

            def expert(e, r):
                need(v, y_full, e - 1)
                for c in range(2, HC):
                    v.wait_ge(h_full, HC * e + c + 1)
                    v.tensor_scalar(hT[r][:, c, :], ps[:, 2 + c, :], b_hid[:, bass.ds(HC * e + c, 1)], 0.0,
                                    ALU.add, ALU.max).then_inc(h_dve, 1)

            def weigh(e, r):
                v.wait_ge(y_full, e + 1)
                need(v, y_out[r], 16 * TT * (half(e)))
                v.tensor_tensor(y[r][:, :, :], ps[:, 6 + r, :].rearrange("p (t c) -> p t c", t=TT),
                                rec_l[r][:, :, C:C + 1].broadcast_to([P, TT, C]), ALU.mult).then_inc(y_done, 1)

            expert(0, 0)
            weigh(0, 0)
            expert(1, 1)
            with v.Fori(1, NE // 2) as i:
                for r in range(2):
                    weigh(2 * i + r - 1, 1 - r)
                    expert(2 * i + r, r)
            weigh(NE - 1, 1)

            def finish(c, r):
                v.wait_ge(f_in[r], 48 * (half(c) + 1))
                v.tensor_tensor(f_s[r][:, :, :], f_y[r][:, 0, :, :], f_y[r][:, 1, :, :], ALU.add).then_inc(f_sum, 1)
                v.wait_ge(f_sum, c + 1)
                need(v, done_out[r], 16 * half(c))
                v.tensor_tensor(f_o[r][:, :, :], f_x[r][:, :, :], f_s[r][:, :, :], ALU.add).then_inc(f_done, 1)

            finish(0, 0)
            finish(1, 1)
            with v.Fori(1, NB // 2) as i:
                finish(2 * i, 0)
                finish(2 * i + 1, 1)

        @block.gpsimd
        def _(pool):
            q = 0

            def quiet(ins):
                nonlocal q
                q += 1
                ins.then_inc(set_q, 1)
                pool.wait_ge(set_q, q)

            set_q = split_m
            quiet(pool.memset(blank[:, :, :], 0.0))
            pool.memset(blank[:, :, C + 1], 1.0e9).then_inc(pool_c, 1)
            for m, dt in ((ident, F32), (identb, BF16)):
                quiet(pool.memset(m[:, :], 0.0))
                quiet(pool.affine_select(out=m[:, :], in_=m[:, :], compare_op=ALU.not_equal, fill=1.0, base=0,
                                         pattern=[[-1, P]], channel_multiplier=1))
            quiet(pool.memset(onesb[:, :], 1.0))
            quiet(pool.memset(ones1[:, :], 1.0))
            pool.affine_select(out=before[:, :], in_=onesb[:, :], compare_op=ALU.is_gt, fill=0.0, base=0,
                               pattern=[[1, P]], channel_multiplier=-1).then_inc(pool_c, 1)
            blocks = w_qv[:, 0, :].rearrange("p (h e) -> p h e", h=NH)
            pool.wait_ge(loaded, 16 * 10)
            quiet(pool.tensor_copy(blocks, w_small[:, :].rearrange("p (a e) -> p a e", a=1).broadcast_to([P, NH, D])))
            quiet(pool.affine_select(out=blocks, in_=blocks, compare_op=ALU.is_ge, fill=0.0, base=0,
                                     pattern=[[-D, NH], [0, D]], channel_multiplier=1))
            quiet(pool.affine_select(out=blocks, in_=blocks, compare_op=ALU.is_ge, fill=0.0, base=D - 1,
                                     pattern=[[D, NH], [0, D]], channel_multiplier=-1))
            quiet(pool.memset(neg_half[:, :], -0.5))
            quiet(pool.iota(falling[:, 0, :], pattern=[[-1, NE]], base=NE, channel_multiplier=0,
                            allow_small_or_imprecise_dtypes=True))
            quiet(pool.iota(slot_base[:, 0, :], pattern=[[CAP, NE]], base=0, channel_multiplier=0,
                            allow_small_or_imprecise_dtypes=True))
            quiet(pool.iota(dest[:, :, :], pattern=[[1, TT], [NTOK, 2]], base=0, channel_multiplier=TT,
                            allow_small_or_imprecise_dtypes=True))
            for i in range(4):
                quiet(pool.memset(qa[i][:, :, :, MROW:STACK], 0.0))
                quiet(pool.memset(ka[i][:, :, :, MROW:STACK], 0.0))
                quiet(pool.memset(ka[i][:, :, :, MROW:MROW + 2], 1.0))
                quiet(pool.memset(ks[i][:, :, :], 0.0))
                quiet(pool.memset(va[i][:, :, :, D:32], 0.0))
                quiet(pool.memset(va[i][:, :, :, D:D + 1], 1.0))
            pool.memset(rest[:, :, :, :, :], 0.0).then_inc(pool_c, 1)
            pool.wait_ge(pool_c, 3)
            SET = q

            def hold(semaphore, count):
                need(pool, semaphore, count)
                if not isinstance(count, int):
                    pool.sem_inc(pool_waits, 1)

            def split(X, gx):
                i = gx % GB
                base = 6 * X
                hold(full["mT"], X - 3)
                hold(full["kT"], X - 3)
                pool.memset(qa[i][:, :, :, MROW:MROW + 2], 0.0)
                for n, (src, dst, first, second) in enumerate((
                        (qv[:, :, 0, :], qa[i], (0, 2, 3), (1, 2, 2)), (z[:, :, :], ka[i], (3, 1, 3), (0, 1, 2)))):
                    s = src.rearrange("p t (h d) -> p t h d", d=D)[:, :, HG * i:HG * i + HG, :]
                    d6 = dst[:, :, :, 0:MROW].rearrange("p t h (a d) -> p (t h) a d", d=D)
                    r = rest[:, n, :, :, :]
                    r3 = r.rearrange("p t h (a d) -> p (t h) a d", a=1)
                    lead = d6[:, :, first[0]:first[0] + first[1] * (first[2] - 1) + 1:first[1], :]
                    mid = d6[:, :, second[0]:second[0] + second[1] * (second[2] - 1) + 1:second[1], :]
                    last = d6[:, :, 5, :] if n == 0 else d6[:, :, 2, :]
                    st = stage[:, n, :, :, :]
                    pool.tensor_scalar(st, s, 1.0, 0.0, ALU.mult, ALU.add).then_inc(split_q, 1)
                    hold(split_q, base + 3 * n + 1)
                    st3 = st.rearrange("p t h (a d) -> p (t h) a d", a=1)
                    pool.tensor_scalar(lead, st3.broadcast_to([P, TT * HG, 3, D]), 1.0, 0.0, ALU.mult, ALU.add)
                    pool.tensor_tensor(r, s, st, ALU.subtract).then_inc(split_q, 1)
                    hold(split_q, base + 3 * n + 2)
                    pool.tensor_scalar(mid, r3.broadcast_to([P, TT * HG, 2, D]), 1.0, 0.0, ALU.mult, ALU.add)\
                        .then_inc(split_q, 1)
                    hold(split_q, base + 3 * n + 3)
                    ins = pool.tensor_tensor(last, r.rearrange("p t h d -> p (t h) d"), mid[:, :, 0, :],
                                             ALU.subtract)
                ins.then_inc(split_done, 1)

            def values(X, gx):
                i = gx % GB
                hold(av_part, TT * (X - 3))
                for tt in range(TT):
                    ins = pool.tensor_tensor(
                        va[i][:, tt, :, 0:D],
                        qv[:, tt, 1, :].rearrange("p (h d) -> p h d", d=D)[:, HG * i:HG * i + HG, :],
                        bv_row[:, :].rearrange("p (h d) -> p h d", d=D)[:, HG * i:HG * i + HG, :], ALU.add)
                ins.then_inc(v_done, 1)

            def maxima(X, gx):
                i = gx % GB
                m = neg_max[gx % 2]
                hold(full["qT"], X + 1)
                hold(max_done, TT * HG * (X + 1))
                pool.tensor_scalar(qa[i][:, :, :, MROW:MROW + 1], m[:, :, :, :], 1.0, 0.0, ALU.mult, ALU.add)\
                    .then_inc(split_m, 1)
                hold(split_m, SET + X + 1)
                pool.tensor_tensor(qa[i][:, :, :, MROW + 1:MROW + 2], m[:, :, :, :],
                                   qa[i][:, :, :, MROW:MROW + 1], ALU.subtract).then_inc(m_done, 1)

            def normalise(mv, ln, sem_q, i, out_of, src, ready):
                pool.tensor_scalar(ln[:, 0, :], mv[:, :, 1], 1.0, EPS, ALU.mult, ALU.add).then_inc(sem_q, 1)
                pool.tensor_scalar(ln[:, 2, :], mv[:, :, 0], -1.0, 0.0, ALU.mult, ALU.add).then_inc(sem_q, 1)
                hold(sem_q, 3 * i + 2)
                pool.tensor_tensor(ln[:, 1, :], ln[:, 0, :], neg_half[:, :], ALU.pow).then_inc(sem_q, 1)
                hold(sem_q, 3 * i + 3)
                for tt in range(TT):
                    ins = pool.tensor_scalar(out_of(tt), src(tt), ln[:, 2, tt:tt + 1], ln[:, 1, tt:tt + 1],
                                             ALU.add, ALU.mult)
                ins.then_inc(ready, 1)

            def batch(b):
                for g in range(GB):
                    G = GB * b + g
                    X, gx = G + 3, g + 3
                    if live(X, NG):
                        if gx % GB == 0:
                            hold(done["qv"], 2 * (b + (g + 3) // GB + 1))
                        hold(z_done, b + (g + 3) // GB + 1)
                        split(X, gx)
                    if live(G + 1, NG):
                        maxima(G + 1, g + 1)
                    if live(X, NG):
                        values(X, gx)
                    if g == 0 and live(b + 1, NB):
                        f = b + 1
                        hold(stat_a_done, f + 1)
                        hold(split_done, GB * f)
                        hold(full["zT"], f)
                        normalise(mv_a, ln_a, ln_q, f, lambda tt: z[:, tt, :], lambda tt: x_a[:, tt, :], z_done)
                    if g == 0 and live(b - 1, NB):
                        k = b - 1
                        hold(xb_in, 16 * b)
                        hold(done["out"], k)
                        pool.tensor_tensor(x_bo[:, :, :], x_b[:, :, :],
                                           bo_row[:, :].rearrange("p (a c) -> p a c", a=1).broadcast_to([P, TT, C]),
                                           ALU.add).then_inc(xbo_done, 1)
                    if g == 1 and live(b - 1, NB):
                        k = b - 1
                        hold(stat_b_done, b)
                        hold(rec_out, 16 * 2 * TT * k)
                        normalise(mv_b, ln_b, ln2_q, k,
                                  lambda tt: rec[:, tt, :, 0:C],
                                  lambda tt: x2[:, tt:tt + 1, :].broadcast_to([P, 2, C]), y_norm)
                        pool.tensor_scalar(rec[:, :, :, C + 1].bitcast(I32), dest[:, :, :], 1.0, 0.0,
                                           ALU.mult, ALU.add).then_inc(dest_q, 1)
                        hold(dest_q, 2 * k + 1)
                        pool.tensor_scalar(dest[:, :, :], dest[:, :, :], 1.0, float(T), ALU.mult, ALU.add)\
                            .then_inc(dest_q, 1)
                        hold(dest_q, 2 * k + 2)
                    if g == 3 and live(b - 1, NB):
                        hold(route_done, b)
                        hold(blank_out, 16 * (1 + 2 * NB))
                        for tt in range(TT):
                            for k in range(2):
                                pool.indirect_dma_start(
                                    out=rec_d, out_offset=bass.IndirectOffsetOnAxis(
                                        ap=slot[:, k, tt, :].bitcast(U32), axis=0),
                                    in_=rec[:, tt, k, :], in_offset=None, bounds_check=NE * CAP - 1,
                                    oob_is_err=False).then_inc(rec_out, 16)

            run_batches(pool, batch)

            def scatter(e, r):
                hold(y_done, e + 1)
                for n in range(TT):
                    pool.indirect_dma_start(
                        out=y_d, out_offset=bass.IndirectOffsetOnAxis(
                            ap=rec_l[r][:, n, C + 1:C + 2].bitcast(U32), axis=0),
                        in_=y[r][:, n, :], in_offset=None, bounds_check=2 * NTOK - 1,
                        oob_is_err=False).then_inc(y_out[r], 16)

            with pool.Fori(0, NE // 2) as i:
                scatter(2 * i, 0)
                scatter(2 * i + 1, 1)


_INS = ['L0_attn_x', 'L0_attn_w_att_val', 'L0_attn_wv_w', 'L0_attn_wv_b', 'L0_attn_out_w', 'L0_attn_out_b',
        'L0_ffn_rw1', 'L0_ffn_rb1', 'L0_ffn_rw2', 'L0_ffn_rb2', 'L0_ffn_ew1', 'L0_ffn_eb1', 'L0_ffn_ew2',
        'L0_ffn_eb2']
_OUTS = [((NB, T, C), 'float32')]


def kernel(**inputs):
    import numpy as _np
    import concourse.bacc as _bacc
    from concourse import mybir as _mybir
    from concourse.bass_utils import run_bass_kernel_spmd as _run

    nc = _bacc.Bacc("TRN2", target_bir_lowering=False, num_devices=1)
    arrays, args = {}, []
    for name in _INS:
        a = _np.ascontiguousarray(inputs[name])
        arrays[f"in_{name}_dram"] = a
        args.append(nc.dram_tensor(f"in_{name}_dram", a.shape, _mybir.dt.from_np(a.dtype), kind="ExternalInput").ap())
    for i, (shape, dtype) in enumerate(_OUTS):
        dt = _mybir.dt.from_np(_np.dtype(dtype))
        args.append(nc.dram_tensor(f"out_{i}_dram", shape, dt, kind="ExternalOutput").ap())
    build(nc, *args)
    r = _run(nc, [arrays], core_ids=[0])
    got = tuple(r.results[0][f"out_{i}_dram"] for i in range(len(_OUTS)))
    return got[0]
```

```python
from contextlib import ExitStack

import concourse.bass as bass
from concourse import mybir

F32 = mybir.dt.float32
BF16 = mybir.dt.bfloat16
I32 = mybir.dt.int32
U32 = mybir.dt.uint32
ALU = mybir.AluOpType
ACT = mybir.ActivationFunctionType
AXIS = mybir.AxisListType

P = 128
NB, T, C = 8, 512, 128
NH, D = 16, 8
TT = T // P
HG = 4
GB = NH // HG
NG = NB * GB
STACK = 64
PARTS = 6
MROW = PARTS * D
NE, CAP, HID = 8, 512, 512
HC = HID // P
NTOK = NB * T
REC = C + 2
SCALE = float(D) ** -0.5
EPS = 1e-5
DROPPED = float(1 << 20)
SLOTS = 8

SHARED = [
    (0, 0, "kT", 2, 0, 0), (0, 2, "qT", 2, 0, 0), (0, 3, "avT", -1, 0, 0), (0, 4, "oT", -1, 1, 0),
    (0, 5, "out", -1, 1, 0), (0, 6, "mT", 1, 0, 0), (0, 7, "zT", 1, 1, 0),
    (1, 0, "kT", 2, 0, 0), (1, 1, "qv", 1, 2, 0), (1, 2, "qT", 2, 0, 0), (1, 3, "avT", -1, 0, 0),
    (1, 4, "qv", 1, 2, 1), (1, 5, "yT", -1, 1, 0), (1, 6, "mT", 1, 0, 0), (1, 7, "hid", -1, 4, 0),
    (2, 0, "kT", 2, 0, 0), (2, 1, "hid", -1, 4, 1), (2, 2, "qT", 2, 0, 0), (2, 3, "avT", -1, 0, 0),
    (2, 4, "hid", -1, 4, 2), (2, 5, "hid", -1, 4, 3), (2, 6, "mT", 1, 0, 0), (2, 7, "logT", -1, 1, 0),
    (3, 0, "logit", -1, 1, 0), (3, 1, "kT", 2, 0, 0), (3, 2, "qT", 2, 0, 0), (3, 3, "avT", -1, 0, 0),
    (3, 4, "rank", -1, 1, 0), (3, 6, "mT", 1, 0, 0),
]
USES = ("kT", "qT", "mT", "avT", "oT", "zT", "qv", "out", "yT", "hid", "logT", "logit", "rank")


def live(i, n):
    return not isinstance(i, int) or 0 <= i < n


def need(eng, sem, count):
    if not isinstance(count, int) or count > 0:
        eng.wait_ge(sem, count)


def use_index(b, use):
    g, _, _, off, per, _ = use
    return b + off if per else GB * b + g + off


def use_exists(b, use):
    return live(use_index(b, use), NB if use[4] else NG)


def use_count(b, use):
    i = use_index(b, use)
    return i * use[4] + use[5] + 1 if use[4] else i + 1


def use_before(b, k):
    for back in range(4):
        for n in reversed(range(k if back == 0 else len(SHARED))):
            if use_exists(b - back, SHARED[n]):
                return SHARED[n][2], use_count(b - back, SHARED[n])
    return None


def half(i):
    return i // 2


def run_batches(eng, body):
    body(-1)
    body(0)
    body(1)
    with eng.Fori(2, NB - 1) as b:
        body(b)
    body(NB - 1)
    body(NB)


def build(nc, x, w_att, wv_w, wv_b, out_w, out_b, rw1, rb1, rw2, rb2, ew1, eb1, ew2, eb2, out):
    rec_d = nc.dram_tensor("dispatched_rows", (NE * CAP, REC), F32).ap()
    y_d = nc.dram_tensor("expert_rows", (2 * NTOK, C), F32).ap()
    x_in = x.rearrange("b (p t) c -> b p t c", t=TT)
    rec_v = rec_d.rearrange("(e p n) r -> e p n r", p=P, n=TT)
    y_v = y_d.rearrange("(k b p t) c -> k b p t c", k=2, p=P, t=TT)
    out_v = out.rearrange("b (p t) c -> b p t c", t=TT)

    with ExitStack() as ctx:
        def sb(name, shape, dt=F32):
            return ctx.enter_context(nc.sbuf_tensor(name, shape, dt))

        def sem(name):
            return ctx.enter_context(nc.semaphore(name))

        ident = sb("ident", [P, P])
        identb = sb("identb", [P, P], BF16)
        before = sb("before", [P, P], BF16)
        onesb = sb("onesb", [P, P], BF16)
        w_small = sb("w_small", [P, D])
        w_qv = sb("w_qv", [P, 2, C])
        w_raw = sb("w_raw", [P, 2, C])
        w_out = sb("w_out", [P, C])
        bv_row = sb("bv_row", [P, C])
        bo_row = sb("bo_row", [P, C])
        b_raw = sb("b_raw", [NE * HC + HC, P])
        b_hid = sb("b_hid", [P, NE * HC + HC])
        rw1_s = sb("rw1_s", [P, HID])
        rw2_s = sb("rw2_s", [P, HC, 32])
        picker = sb("picker", [P, NE])
        rb2_row = sb("rb2_row", [P, NE])
        neg_half = sb("neg_half", [P, TT])
        falling = sb("falling", [P, 1, NE])
        slot_base = sb("slot_base", [P, 1, NE])
        x_a = sb("x_a", [P, TT, C])
        x_b = sb("x_b", [P, TT, C])
        x_bo = sb("x_bo", [P, TT, C])
        stat_a = sb("stat_a", [P, TT, 6])
        mv_a = sb("mv_a", [P, TT, 2])
        ln_a = sb("ln_a", [P, 3, TT])
        z = sb("z", [P, TT, C])
        zT = sb("zT", [P, T])
        qv = sb("qv", [P, TT, 2, C])
        stage = sb("stage", [P, 2, TT, HG, D], BF16)
        rest = sb("rest", [P, 2, TT, HG, D])
        qa = [sb(f"qa{i}", [P, TT, HG, STACK], BF16) for i in range(4)]
        ka = [sb(f"ka{i}", [P, TT, HG, STACK], BF16) for i in range(4)]
        va = [sb(f"va{i}", [P, TT, HG, 32]) for i in range(4)]
        ks = [sb(f"ks{i}", [P, HG, T], BF16) for i in range(4)]
        qs = [sb(f"qs{i}", [P, 2, T], BF16) for i in range(2)]
        qm = [sb(f"qm{i}", [P, 2, T], BF16) for i in range(2)]
        neg_max = [sb(f"neg_max{i}", [P, TT, HG, 1]) for i in range(2)]
        probs = sb("probs", [P, TT, HG, T])
        av = sb("av", [P, T])
        inv_sum = sb("inv_sum", [P, TT, HG, 1])
        o_tok = sb("o_tok", [P, TT, NH, D])
        oT = sb("oT", [P, T])
        x2 = sb("x2", [P, TT, C])
        x2_all = sb("x2_all", [P, NB, TT, C])
        stat_b = sb("stat_b", [P, TT, 6])
        mv_b = sb("mv_b", [P, TT, 2])
        ln_b = sb("ln_b", [P, 3, TT])
        rec = sb("rec", [P, TT, 2, REC])
        yT = sb("yT", [P, T])
        hid = sb("hid", [P, HC, T])
        logT = sb("logT", [P, T])
        logits = sb("logits", [P, TT, NE])
        tmp = sb("tmp", [P, TT, NE])
        top = sb("top", [P, 2, TT, 1])
        pick = sb("pick", [P, 2, TT, 1])
        chosen = sb("chosen", [P, 2, TT, NE])
        mask = sb("mask", [P, TT, NE], BF16)
        gap = sb("gap", [P, TT])
        e_gap = sb("e_gap", [P, TT])
        den = sb("den", [P, TT])
        taken = sb("taken", [P, NE])
        pos = sb("pos", [P, TT, NE])
        over = sb("over", [P, TT, NE])
        addr = sb("addr", [P, 1, TT, NE])
        slot_e = sb("slot_e", [P, 2, TT, NE])
        slot_f = sb("slot_f", [P, 2, TT, 1])
        slot = sb("slot", [P, 2, TT, 1], I32)
        dest = sb("dest", [P, TT, 2])
        blank = sb("blank", [P, 1, TT, REC])
        rec_l = [sb(f"rec_l{i}", [P, TT, REC]) for i in range(2)]
        w1 = [sb(f"w1_{i}", [P, HID]) for i in range(2)]
        w2 = [sb(f"w2_{i}", [P, HC, C]) for i in range(2)]
        b2 = [sb(f"b2_{i}", [P, 1, C]) for i in range(2)]
        meta = [sb(f"meta{i}", [P, TT, 2]) for i in range(2)]
        yb = sb("yb", [P, TT, C])
        xT = [sb(f"xT{i}", [P, CAP]) for i in range(2)]
        hT = [sb(f"hT{i}", [P, HC, CAP]) for i in range(2)]
        y = [sb(f"y{i}", [P, TT, C]) for i in range(2)]
        f_y = [probs[:, i, 0:2, :].rearrange("p k (t c) -> p k t c", t=TT) for i in range(2)]
        f_s = [probs[:, i, 2, :].rearrange("p (t c) -> p t c", t=TT) for i in range(2)]
        f_o = [probs[:, i, 3, :].rearrange("p (t c) -> p t c", t=TT) for i in range(2)]

        ps = ctx.enter_context(nc.psum_tensor("ps", [P, 8, 512], F32))
        score = [ps[:, 0:2, :], ps[:, 2:4, :]]
        plain = [ps[:, 4, :], ps[:, 5, :]]
        acc = ps[:, 6, :]
        shared = ps[:, 7, :]
        shared_b = shared.bitcast(BF16)

        loaded = sem("loaded")
        xa_in, xb_in, x2_out = sem("xa_in"), sem("xb_in"), sem("x2_out")
        blank_out, rec_out = sem("blank_out"), sem("rec_out")
        pool_c, dve_c, act_c, pe_c = sem("pool_c"), sem("dve_c"), sem("act_c"), sem("pe_c")
        pool_waits, dve_waits = sem("pool_waits"), sem("dve_waits")
        kT_done_2 = sem("kT_done_2")
        full = {n: sem(f"{n}_full") for n in USES}
        done = {n: sem(f"{n}_done") for n in USES}
        score_full, exp_done = sem("score_full"), sem("exp_done")
        plain_full, max_done = sem("plain_full"), sem("max_done")
        av_part, av_out = sem("av_part"), sem("av_out")
        split_done, v_done, m_done = sem("split_done"), sem("v_done"), sem("m_done")
        stat_a_done, z_done = sem("stat_a_done"), sem("z_done")
        xbo_done, stat_b_done, y_norm = sem("xbo_done"), sem("stat_b_done"), sem("y_norm")
        gap_done, egap_done, mask_done, route_done = (sem("gap_done"), sem("egap_done"), sem("mask_done"),
                                                      sem("route_done"))
        split_q, split_m, ln_q, ln2_q, dest_q = (sem("split_q"), sem("split_m"), sem("ln_q"), sem("ln2_q"),
                                                 sem("dest_q"))
        st_q, st2_q, inv_q, route_q = sem("st_q"), sem("st2_q"), sem("inv_q"), sem("route_q")
        def two(name):
            return [sem(f"{name}{r}") for r in range(2)]

        w_in, rl_in, y_out = two("w_in"), two("rl_in"), two("y_out")
        xT_full, xT_done = sem("xT_full"), sem("xT_done")
        h_full, h_act, h_dve = sem("h_full"), sem("h_act"), sem("h_dve")
        y_full, y_bias, y_done, meta_done = sem("y_full"), sem("y_bias"), sem("y_done"), sem("meta_done")
        f_in, done_out = two("f_in"), two("done_out")
        f_sum, f_done = sem("f_sum"), sem("f_done")

        block = ctx.enter_context(nc.Block())

        @block.sync
        def _(sp):
            def load(dst, src):
                sp.dma_start(dst, src).then_inc(loaded, 16)

            sp.dma_start(x_a[:, :, :], x_in[0]).then_inc(xa_in, 16)
            load(w_small[:, :], w_att.rearrange("h d e -> (h d) e"))
            load(w_raw[:, 0, :], wv_w)
            load(w_raw[:, 1, :], out_w)
            load(b_raw[0:NE * HC, :], eb1.rearrange("e (c p) -> (e c) p", p=P))
            load(b_raw[NE * HC:NE * HC + HC, :], rb1.rearrange("(c p) -> c p", p=P))
            load(bv_row[:, :], wv_b.rearrange("(a c) -> a c", a=1).broadcast_to([P, C]))
            load(bo_row[:, :], out_b.rearrange("(a c) -> a c", a=1).broadcast_to([P, C]))
            load(rb2_row[:, :], rb2.rearrange("(a c) -> a c", a=1).broadcast_to([P, NE]))
            load(rw1_s[:, :], rw1)
            sp.wait_ge(pool_c, 1)
            load(rw2_s[:, :, 0:NE], rw2.rearrange("(c p) e -> p c e", p=P))
            sp.dma_start(rec_d.rearrange("(p e n) r -> p e n r", p=P, n=TT),
                         blank[:, :, :, :].broadcast_to([P, NE, TT, REC])).then_inc(blank_out, 16)
            for k in range(2):
                for b in range(NB):
                    sp.dma_start(y_v[k, b], blank[:, 0, :, 0:C]).then_inc(blank_out, 16)

            def batch(b):
                f, k = b + 1, b - 1
                if live(f, NB):
                    if not isinstance(f, int) or f > 0:
                        need(sp, z_done, f)
                        sp.dma_start(x_a[:, :, :], x_in[f]).then_inc(xa_in, 16)
                if live(b, NB):
                    need(sp, xbo_done, b)
                    sp.dma_start(x_b[:, :, :], x_in[b]).then_inc(xb_in, 16)
                if live(k, NB):
                    sp.wait_ge(done["out"], k + 1)
                    sp.dma_start(x2_all[:, bass.ds(k, 1), :, :], x2[:, :, :]).then_inc(x2_out, 16)

            def weights_2(e, r):
                sp.dma_start(w2[r][:, :, :], ew2[e].rearrange("(c p) n -> p c n", p=P)).then_inc(w_in[r], 16)
                sp.dma_start(b2[r][:, :, :], eb2[bass.ds(e, 1), :].rearrange("(a b) c -> a b c", a=1)
                             .broadcast_to([P, 1, C])).then_inc(w_in[r], 16)

            for r in range(2):
                sp.dma_start(w1[r][:, :], ew1[r]).then_inc(w_in[r], 16)
                weights_2(r, r)
            run_batches(sp, batch)

            def rows(e, r):
                need(sp, xT_full, e - 1)
                need(sp, meta_done, e - 1)
                sp.dma_start(rec_l[r][:, :, :], rec_v[e]).then_inc(rl_in[r], 16)

            def expert(e, r):
                rows(e, r)
                need(sp, h_full, HC * (e - 1))
                sp.dma_start(w1[r][:, :], ew1[e]).then_inc(w_in[r], 16)
                need(sp, y_bias, e - 1)
                weights_2(e, r)

            sp.wait_ge(rec_out, 16 * 2 * TT * NB)
            rows(0, 0)
            rows(1, 1)
            with sp.Fori(1, NE // 2) as i:
                expert(2 * i, 0)
                expert(2 * i + 1, 1)

            def finish(c, r):
                need(sp, f_sum, c - 1)
                sp.dma_start(f_y[r][:, 0, :, :], y_v[0, c]).then_inc(f_in[r], 16)
                sp.dma_start(f_y[r][:, 1, :, :], y_v[1, c]).then_inc(f_in[r], 16)

            for r in range(2):
                sp.wait_ge(y_out[r], 16 * TT * NE // 2)
            finish(0, 0)
            finish(1, 1)
            with sp.Fori(1, NB // 2) as i:
                finish(2 * i, 0)
                finish(2 * i + 1, 1)
            for r in range(2):
                sp.wait_ge(done_out[r], 16 * NB // 2)

        @block.tensor
        def _(pe):
            pe.wait_ge(loaded, 16 * 10)
            pe.wait_ge(pool_c, 2)
            pe.transpose(ps[:, 0, 0:P], w_raw[:, 0, :], ident[:, :])
            pe.transpose(ps[:, 0, P:2 * P], w_raw[:, 1, :], ident[:, :])
            pe.transpose(ps[:, 0, 2 * P:2 * P + NE * HC + HC], b_raw[:, :],
                         ident[0:NE * HC + HC, 0:NE * HC + HC]).then_inc(pe_c, 1)
            pe.wait_ge(act_c, 1)
            pe.wait_ge(pool_c, 3)

            def scores(G, g, j):
                st, pair = j // 2, j % 2
                if j == 0:
                    need(pe, done["mT"], G + 1)
                need(pe, exp_done, SLOTS * G + j - 1)
                for i in range(2):
                    mm = pe.matmul(score[j % 2][:, i, :], ks[g][:, 2 * pair + i, st * P:(st + 1) * P],
                                   qm[g % 2][:, pair, :], start=True, stop=True)
                mm.then_inc(score_full, 1)

            def values(G, g, st):
                if st == 0:
                    need(pe, av_out, G)
                    need(pe, v_done, G + 1)
                need(pe, exp_done, SLOTS * G + 2 * st + 2)
                for h in range(HG):
                    mm = pe.matmul(acc[32 * h:32 * h + 32, :], va[g][:, st, h, :], probs[:, st, h, :],
                                   start=(st == 0), stop=(st == TT - 1))
                mm.then_inc(av_part, 1)

            def plain_scores(X, gx, u):
                tt, h = u // HG, u % HG
                if u == 0:
                    need(pe, done["kT"], X + 1)
                    need(pe, kT_done_2, X + 1)
                    need(pe, done["qT"], X + 1)
                need(pe, max_done, TT * HG * X + u - 1)
                pe.matmul(plain[u % 2], qs[gx % 2][:, h // 2, tt * P:(tt + 1) * P],
                          ks[gx % 4][:, h, :], start=True, stop=True).then_inc(plain_full, 1)

            def stack_transposes(src):
                for pair in range(2):
                    for tt in range(TT):
                        n = pair * TT + tt
                        mm = pe.transpose(shared_b[:, n * P:(n + 1) * P],
                                          src[:, tt, 2 * pair:2 * pair + 2, :].rearrange("p h c -> p (h c)"),
                                          identb[:, :])
                return mm

            def token_transposes(tile):
                for tt in range(TT):
                    mm = pe.transpose(shared[:, tt * P:(tt + 1) * P], tile(tt), ident[:, :])
                return mm

            def shared_use(b, k):
                g, _, name, off, _, o = SHARED[k]
                i = use_index(b, SHARED[k])
                prior = use_before(b, k)
                if prior:
                    need(pe, done[prior[0]], prior[1])
                    if prior[0] == "kT":
                        need(pe, kT_done_2, prior[1])
                if name == "kT":
                    need(pe, split_done, i + 1)
                    mm = stack_transposes(ka[(g + off) % 4])
                elif name == "qT":
                    mm = stack_transposes(qa[(g + off) % 4])
                elif name == "mT":
                    need(pe, m_done, i + 1)
                    mm = stack_transposes(qa[(g + off) % 4])
                elif name == "avT":
                    need(pe, av_out, i + 1)
                    mm = token_transposes(lambda tt: av[:, tt * P:(tt + 1) * P])
                elif name == "oT":
                    need(pe, done["avT"], GB * (i + 1))
                    mm = token_transposes(lambda tt: o_tok[:, tt, :, :].rearrange("p h d -> p (h d)"))
                elif name == "zT":
                    need(pe, z_done, i + 1)
                    mm = token_transposes(lambda tt: z[:, tt, :])
                elif name == "yT":
                    need(pe, y_norm, i + 1)
                    mm = token_transposes(lambda tt: rec[:, tt, 0, 0:C])
                elif name == "qv":
                    need(pe, done["zT"], i + 1)
                    for n in range(2):
                        tt = 2 * o + n
                        mm = pe.matmul(shared[:, n * 2 * C:(n + 1) * 2 * C], zT[:, tt * P:(tt + 1) * P],
                                       w_qv[:, :, :].rearrange("p a c -> p (a c)"), start=True, stop=True)
                elif name == "out":
                    need(pe, done["oT"], i + 1)
                    for tt in range(TT):
                        mm = pe.matmul(shared[:, tt * C:(tt + 1) * C], oT[:, tt * P:(tt + 1) * P], w_out[:, :],
                                       start=True, stop=True)
                elif name == "hid":
                    need(pe, done["yT"], i + 1)
                    mm = pe.matmul(shared, rw1_s[:, o * P:(o + 1) * P], yT[:, :], start=True, stop=True)
                elif name == "logT":
                    need(pe, done["hid"], HC * (i + 1))
                    for c in range(HC):
                        mm = pe.matmul(shared[32 * c:32 * c + 32, :], rw2_s[:, c, :], hid[:, c, :],
                                       start=True, stop=True)
                elif name == "logit":
                    need(pe, done["logT"], i + 1)
                    for tt in range(TT):
                        mm = pe.matmul(shared[:, tt * NE:(tt + 1) * NE], logT[:, tt * P:(tt + 1) * P],
                                       picker[:, :], start=True, stop=True)
                elif name == "rank":
                    need(pe, mask_done, i + 1)
                    for n, w in enumerate((before, onesb)):
                        for tt in range(TT):
                            mm = pe.matmul(shared[:, n * NE:(n + 1) * NE], w[:, :], mask[:, tt, :],
                                           start=(tt == 0), stop=(tt == TT - 1))
                mm.then_inc(full[name], 1)

            def batch(b):
                for g in range(GB):
                    G = GB * b + g
                    for j in range(SLOTS):
                        if live(G, NG):
                            scores(G, g, j)
                        X, gx = (G + 1, g + 1) if j < 4 else (G + 2, g + 2)
                        if live(X, NG):
                            for u in range(2):
                                plain_scores(X, gx, (2 * j + 8) % 16 + u)
                        if j == 1 and live(G - 1, NG):
                            values(G - 1, (g - 1) % 4, 3)
                        if j >= 3 and j % 2 and live(G, NG):
                            values(G, g, (j - 3) // 2)
                        for k, use in enumerate(SHARED):
                            if use[0:2] == (g, j) and use_exists(b, use):
                                shared_use(b, k)

            run_batches(pe, batch)

            def rows_T(e, r):
                pe.wait_ge(rl_in[r], 16 * (half(e) + 1))
                need(pe, xT_done, e - 1)
                for n in range(TT):
                    mm = pe.transpose(ps[:, r, n * P:(n + 1) * P], rec_l[r][:, n, 0:C], ident[:, :])
                mm.then_inc(xT_full, 1)

            def first(e, r):
                pe.wait_ge(w_in[r], 48 * (half(e) + 1))
                pe.wait_ge(xT_done, e + 1)
                for c in range(HC):
                    need(pe, h_act if c < 2 else h_dve, 2 * (e - 1) + c % 2 + 1)
                    pe.matmul(ps[:, 2 + c, :], w1[r][:, c * P:(c + 1) * P], xT[r][:, :],
                              start=True, stop=True).then_inc(h_full, 1)

            def second(e, r):
                pe.wait_ge(h_act, 2 * (e + 1))
                pe.wait_ge(h_dve, 2 * (e + 1))
                need(pe, y_bias, e - 1)
                for n in range(TT):
                    o = ps[:, 6 + r, n * C:(n + 1) * C]
                    for c in range(HC):
                        mm = pe.matmul(o, hT[r][:, c, n * P:(n + 1) * P], w2[r][:, c, :],
                                       start=(c == 0), stop=(c == HC - 1))
                mm.then_inc(y_full, 1)

            pe.wait_ge(exp_done, SLOTS * NG)
            pe.wait_ge(max_done, TT * HG * NG)
            pe.wait_ge(av_out, NG)
            pe.wait_ge(done["rank"], NB)
            rows_T(0, 0)
            first(0, 0)
            rows_T(1, 1)
            second(0, 0)
            first(1, 1)
            with pe.Fori(1, NE // 2) as i:
                for r in range(2):
                    rows_T(2 * i + r, r)
                    second(2 * i + r - 1, 1 - r)
                    first(2 * i + r, r)
            second(NE - 1, 1)

        @block.scalar
        def _(act):
            act.wait_ge(pe_c, 1)
            act.activation(w_qv[:, 1, :], ps[:, 0, 0:P], ACT.Copy)
            act.activation(w_out[:, :], ps[:, 0, P:2 * P], ACT.Copy)
            act.activation(b_hid[:, :], ps[:, 0, 2 * P:2 * P + NE * HC + HC], ACT.Copy).then_inc(act_c, 1)
            act.wait_ge(act_c, 1)

            def exps(G, j):
                st, pair = j // 2, j % 2
                act.wait_ge(score_full, SLOTS * G + j + 1)
                need(act, av_part, TT * (G - 1) + st + 1)
                act.activation(probs[:, st, 2 * pair:2 * pair + 2, :], score[j % 2], ACT.Exp,
                               scale=SCALE).then_inc(exp_done, 1)

            def read_out(b, use):
                g, _, name, off, _, o = use
                i = use_index(b, use)
                dst, src, func, bias = None, shared, ACT.Copy, 0.0
                if name == "kT":
                    dst = ks[(g + off) % 4][0:STACK, 0:HG:2, :]
                    src = shared_b[0:STACK, :].rearrange("p (a t) -> p a t", a=2)
                    need(act, score_full, SLOTS * (i - 3))
                elif name == "qT":
                    dst, src = qs[(g + off) % 2][:, :, :].rearrange("p a t -> p (a t)"), shared_b
                    need(act, plain_full, TT * HG * (i - 1))
                elif name == "oT":
                    dst = oT[:, :]
                    need(act, full["out"], i)
                elif name == "zT":
                    dst = zT[:, :]
                    need(act, full["qv"], 2 * i)
                elif name == "yT":
                    dst = yT[:, :]
                    need(act, full["hid"], HC * i)
                elif name == "qv":
                    dst = qv[:, 2 * o:2 * o + 2, :, :].rearrange("p t a c -> p (t a c)")
                    need(act, split_done, GB * i)
                    need(act, v_done, GB * i)
                elif name == "hid":
                    dst, func, bias = hid[:, o, :], ACT.Relu, b_hid[:, NE * HC + o:NE * HC + o + 1]
                    need(act, full["logT"], i)
                elif name == "logT":
                    dst = logT[:, :]
                    need(act, full["logit"], i)
                else:
                    return
                act.wait_ge(full[name], use_count(b, use))
                act.activation(dst, src, func, bias=bias).then_inc(done[name], 1)

            def batch(b):
                for g in range(GB):
                    G = GB * b + g
                    for j in range(SLOTS):
                        if live(G, NG):
                            exps(G, j)
                        if j == 1 and live(G - 1, NG):
                            act.wait_ge(av_part, TT * G)
                            need(act, full["avT"], G - 1)
                            act.activation(av[:, :], acc, ACT.Copy).then_inc(av_out, 1)
                        for use in SHARED:
                            if use[0:2] == (g, j) and use_exists(b, use):
                                read_out(b, use)
                        if (g, j) == (3, 3) and live(b - 1, NB):
                            act.wait_ge(gap_done, b)
                            act.activation(e_gap[:, :], gap[:, :], ACT.Exp).then_inc(egap_done, 1)

            run_batches(act, batch)

            def expert(e, r):
                act.wait_ge(xT_full, e + 1)
                act.activation(xT[r][:, :], ps[:, r, :], ACT.Copy).then_inc(xT_done, 1)
                need(act, y_full, e - 1)
                for c in range(2):
                    act.wait_ge(h_full, HC * e + c + 1)
                    act.activation(hT[r][:, c, :], ps[:, 2 + c, :], ACT.Relu,
                                   bias=b_hid[:, bass.ds(HC * e + c, 1)]).then_inc(h_act, 1)

            expert(0, 0)
            expert(1, 1)
            with act.Fori(1, NE // 2) as i:
                expert(2 * i, 0)
                expert(2 * i + 1, 1)

            def store(c, r):
                act.wait_ge(f_done, c + 1)
                act.dma_start(out_v[c], f_o[r][:, :, :]).then_inc(done_out[r], 16)

            with act.Fori(0, NB // 2) as i:
                store(2 * i, 0)
                store(2 * i + 1, 1)

        @block.vector
        def _(v):
            v.memset(taken[:, :], 0.0).then_inc(dve_c, 1)
            v.wait_ge(dve_c, 1)
            v.wait_ge(loaded, 16 * 10)
            v.wait_ge(pool_c, 3)

            def statistics(part, src, stat, mv, q, i, ready):
                if part < 2:
                    for tt in (2 * part, 2 * part + 1):
                        v.bn_stats(stat[:, tt, :], src[:, tt, :]).then_inc(q, 1)
                    return
                for tt in range(TT):
                    v.wait_ge(q, TT * i + tt + 1)
                    if not isinstance(i, int):
                        v.sem_inc(dve_waits, 1)
                    a = v.bn_aggr(mv[:, tt, :], stat[:, tt, :])
                a.then_inc(ready, 1)

            def read_out(b, use):
                g, _, name, off, _, o = use
                i = use_index(b, use)
                if name == "kT":
                    need(v, score_full, SLOTS * (i - 3))
                    v.wait_ge(full["kT"], i + 1)
                    v.tensor_copy(ks[(g + off) % 4][STACK:P, 1:HG:2, :],
                                  shared_b[STACK:P, :].rearrange("p (a t) -> p a t", a=2)).then_inc(kT_done_2, 1)
                elif name == "mT":
                    need(v, score_full, SLOTS * (i - 1))
                    v.wait_ge(full["mT"], i + 1)
                    v.tensor_copy(qm[(g + off) % 2][:, :, :].rearrange("p a t -> p (a t)"), shared_b)\
                     .then_inc(done["mT"], 1)
                elif name == "avT":
                    t4 = shared.rearrange("p (t h c) -> p t h c", t=TT, h=HG)
                    v.wait_ge(full["avT"], i + 1)
                    v.reciprocal(inv_sum[:, :, :, :], t4[:, :, :, D:D + 1]).then_inc(inv_q, 1)
                    v.wait_ge(inv_q, i + 1)
                    if (g + off) % GB == 0:
                        need(v, full["oT"], b + (g + off) // GB)
                    h0 = HG * ((g + off) % GB)
                    v.tensor_tensor(o_tok[:, :, h0:h0 + HG, :], t4[:, :, :, 0:D],
                                    inv_sum[:, :, :, :].broadcast_to([P, TT, HG, D]), ALU.mult)\
                     .then_inc(done["avT"], 1)
                elif name == "out":
                    v.wait_ge(xbo_done, i + 1)
                    need(v, x2_out, 16 * i)
                    need(v, y_norm, i)
                    v.wait_ge(full["out"], i + 1)
                    v.tensor_tensor(x2[:, :, :].rearrange("p t c -> p (t c)"), shared,
                                    x_bo[:, :, :].rearrange("p t c -> p (t c)"), ALU.add)\
                     .then_inc(done["out"], 1)

            CHAIN = 24

            def route(i, h):
                n = CHAIN * i + (0, 0, 1, 3, 5, 7, 9, 11, 11, 13, 15, 15, 17, 19, 21, 23)[h]

                def step(ins):
                    nonlocal n
                    n += 1
                    ins.then_inc(route_q, 1)

                def last():
                    v.wait_ge(route_q, n)

                def largest(k):
                    step(v.tensor_reduce(top[:, k, :, :], logits[:, :, :], AXIS.X, ALU.max))

                def at_largest(k):
                    step(v.tensor_tensor(tmp[:, :, :], logits[:, :, :], top[:, k, :, :].broadcast_to([P, TT, NE]),
                                         ALU.is_equal))

                def numbered(k):
                    step(v.tensor_tensor(tmp[:, :, :], tmp[:, :, :], falling[:, :, :].broadcast_to([P, TT, NE]),
                                         ALU.mult))

                def first_place(k):
                    step(v.tensor_reduce(pick[:, k, :, :], tmp[:, :, :], AXIS.X, ALU.max))

                def one_hot(k):
                    step(v.tensor_tensor(chosen[:, k, :, :], falling[:, :, :].broadcast_to([P, TT, NE]),
                                         pick[:, k, :, :].broadcast_to([P, TT, NE]), ALU.is_equal))

                if h == 1:
                    v.wait_ge(full["logit"], i + 1)
                    need(v, egap_done, i)
                    v.tensor_tensor(logits[:, :, :], shared[:, 0:TT * NE].rearrange("p (t e) -> p t e", t=TT),
                                    rb2_row[:, :].rearrange("p (a e) -> p a e", a=1).broadcast_to([P, TT, NE]),
                                    ALU.add).then_inc(done["logit"], 1)
                    v.wait_ge(done["logit"], i + 1)
                    largest(0)
                elif h == 2:
                    last()
                    at_largest(0)
                    last()
                    numbered(0)
                elif h == 3:
                    last()
                    first_place(0)
                    last()
                    one_hot(0)
                elif h == 4:
                    last()
                    step(v.scalar_tensor_tensor(out=logits[:, :, :], in0=chosen[:, 0, :, :], scalar=-3.0e38,
                                                in1=logits[:, :, :], op0=ALU.mult, op1=ALU.add))
                    last()
                    largest(1)
                elif h == 5:
                    last()
                    v.tensor_tensor(gap[:, :], top[:, 1, :, 0], top[:, 0, :, 0], ALU.subtract)\
                     .then_inc(gap_done, 1)
                    at_largest(1)
                    last()
                    numbered(1)
                elif h == 6:
                    last()
                    first_place(1)
                    last()
                    one_hot(1)
                elif h == 7:
                    last()
                    need(v, full["rank"], i)
                    v.tensor_tensor(mask[:, :, :], chosen[:, 0, :, :], chosen[:, 1, :, :], ALU.add)\
                     .then_inc(mask_done, 1)
                elif h == 8:
                    v.wait_ge(egap_done, i + 1)
                    step(v.tensor_scalar(den[:, :], e_gap[:, :], 1.0, None, ALU.add))
                    last()
                    step(v.reciprocal(den[:, :], den[:, :]))
                elif h == 9:
                    last()
                    need(v, rec_out, 16 * 2 * TT * i)
                    step(v.tensor_copy(rec[:, :, 0, C], den[:, :]))
                    step(v.tensor_tensor(rec[:, :, 1, C], e_gap[:, :], den[:, :], ALU.mult))
                elif h == 10:
                    v.wait_ge(full["rank"], i + 1)
                    v.tensor_tensor(pos[:, 0, :], shared[:, 0:NE], taken[:, :], ALU.add)
                    v.tensor_tensor(taken[:, :], shared[:, NE:2 * NE], taken[:, :], ALU.add)\
                     .then_inc(done["rank"], 1)
                elif h == 11:
                    v.wait_ge(done["rank"], i + 1)
                    step(v.tensor_tensor(pos[:, 1, :], pos[:, 0, :], mask[:, 0, :], ALU.add))
                    last()
                    step(v.tensor_tensor(pos[:, 2, :], pos[:, 1, :], mask[:, 1, :], ALU.add))
                elif h == 12:
                    last()
                    step(v.tensor_tensor(pos[:, 3, :], pos[:, 2, :], mask[:, 2, :], ALU.add))
                    last()
                    step(v.tensor_scalar(over[:, :, :], pos[:, :, :], float(CAP), DROPPED, ALU.is_ge, ALU.mult))
                elif h == 13:
                    last()
                    step(v.tensor_tensor(over[:, :, :], over[:, :, :], pos[:, :, :], ALU.add))
                    last()
                    step(v.tensor_tensor(addr[:, 0, :, :], over[:, :, :],
                                         slot_base[:, :, :].broadcast_to([P, TT, NE]), ALU.add))
                elif h == 14:
                    last()
                    for k in range(2):
                        step(v.tensor_tensor(slot_e[:, k, :, :], chosen[:, k, :, :], addr[:, 0, :, :], ALU.mult))
                elif h == 15:
                    last()
                    step(v.tensor_reduce(slot_f[:, :, :, :], slot_e[:, :, :, :], AXIS.X, ALU.add))
                    last()
                    v.tensor_copy(slot[:, :, :, :], slot_f[:, :, :, :]).then_inc(route_done, 1)

            def maximum(X, gx, u):
                if u == 0:
                    need(v, m_done, X - 1)
                v.wait_ge(plain_full, TT * HG * X + u + 1)
                v.tensor_reduce(neg_max[gx % 2][:, u // HG, u % HG, :], plain[u % 2], AXIS.X,
                                ALU.max, negate=True).then_inc(max_done, 1)

            def side_work(b, g, h):
                if g == 0 and live(b + 1, NB) and h < 3:
                    if h == 0:
                        v.wait_ge(xa_in, 16 * (b + 2))
                        need(v, z_done, b + 1)
                    statistics(h, x_a, stat_a, mv_a, st_q, b + 1, stat_a_done)
                if g == 0 and live(b - 1, NB) and 12 <= h < 15:
                    if h == 12:
                        v.wait_ge(done["out"], b)
                    statistics(h - 12, x2, stat_b, mv_b, st2_q, b - 1, stat_b_done)
                if g == 3 and live(b - 1, NB) and h > 0:
                    route(b - 1, h)

            def batch(b):
                for g in range(GB):
                    G = GB * b + g
                    for j in range(SLOTS):
                        X, gx = (G + 1, g + 1) if j < 4 else (G + 2, g + 2)
                        if live(X, NG):
                            maximum(X, gx, (2 * j + 8) % 16)
                        side_work(b, g, 2 * j)
                        if live(X, NG):
                            maximum(X, gx, (2 * j + 8) % 16 + 1)
                        side_work(b, g, 2 * j + 1)
                        for use in SHARED:
                            if use[0:2] == (g, j) and use_exists(b, use):
                                read_out(b, use)

            run_batches(v, batch)

            def expert(e, r):
                need(v, y_full, e - 1)
                for c in range(2, HC):
                    v.wait_ge(h_full, HC * e + c + 1)
                    v.tensor_scalar(hT[r][:, c, :], ps[:, 2 + c, :], b_hid[:, bass.ds(HC * e + c, 1)], 0.0,
                                    ALU.add, ALU.max).then_inc(h_dve, 1)

            def weigh(e, r):
                v.wait_ge(y_full, e + 1)
                need(v, y_done, e)
                v.tensor_tensor(yb[:, :, :], ps[:, 6 + r, :].rearrange("p (t c) -> p t c", t=TT),
                                b2[r][:, :, :].broadcast_to([P, TT, C]), ALU.add).then_inc(y_bias, 1)
                need(v, y_out[r], 16 * TT * (half(e)))
                v.wait_ge(y_bias, e + 1)
                v.wait_ge(meta_done, e + 1)
                v.tensor_tensor(y[r][:, :, :], yb[:, :, :], meta[r][:, :, 0:1].broadcast_to([P, TT, C]),
                                ALU.mult).then_inc(y_done, 1)

            expert(0, 0)
            weigh(0, 0)
            expert(1, 1)
            with v.Fori(1, NE // 2) as i:
                for r in range(2):
                    weigh(2 * i + r - 1, 1 - r)
                    expert(2 * i + r, r)
            weigh(NE - 1, 1)

            v.wait_ge(x2_out, 16 * NB)

            def finish(c, r):
                v.wait_ge(f_in[r], 32 * (half(c) + 1))
                v.tensor_tensor(f_s[r][:, :, :], f_y[r][:, 0, :, :], f_y[r][:, 1, :, :], ALU.add).then_inc(f_sum, 1)
                v.wait_ge(f_sum, c + 1)
                need(v, done_out[r], 16 * half(c))
                v.tensor_tensor(f_o[r][:, :, :], x2_all[:, bass.ds(c, 1), :, :].rearrange("p a t c -> p (a t) c"),
                                f_s[r][:, :, :], ALU.add).then_inc(f_done, 1)

            finish(0, 0)
            finish(1, 1)
            with v.Fori(1, NB // 2) as i:
                finish(2 * i, 0)
                finish(2 * i + 1, 1)

        @block.gpsimd
        def _(pool):
            q = 0

            def quiet(ins):
                nonlocal q
                q += 1
                ins.then_inc(set_q, 1)
                pool.wait_ge(set_q, q)

            set_q = split_m
            quiet(pool.memset(blank[:, :, :, :], 0.0))
            quiet(pool.memset(rw2_s[:, :, :], 0.0))
            pool.memset(blank[:, :, :, C + 1], 1.0e9).then_inc(pool_c, 1)
            for m, dt in ((ident, F32), (identb, BF16)):
                quiet(pool.memset(m[:, :], 0.0))
                quiet(pool.affine_select(out=m[:, :], in_=m[:, :], compare_op=ALU.not_equal, fill=1.0, base=0,
                                         pattern=[[-1, P]], channel_multiplier=1))
            quiet(pool.memset(onesb[:, :], 1.0))
            pool.affine_select(out=before[:, :], in_=onesb[:, :], compare_op=ALU.is_gt, fill=0.0, base=0,
                               pattern=[[1, P]], channel_multiplier=-1).then_inc(pool_c, 1)
            blocks = w_qv[:, 0, :].rearrange("p (h e) -> p h e", h=NH)
            pool.wait_ge(loaded, 16 * 10)
            quiet(pool.tensor_copy(blocks, w_small[:, :].rearrange("p (a e) -> p a e", a=1).broadcast_to([P, NH, D])))
            quiet(pool.affine_select(out=blocks, in_=blocks, compare_op=ALU.is_ge, fill=0.0, base=0,
                                     pattern=[[-D, NH], [0, D]], channel_multiplier=1))
            quiet(pool.affine_select(out=blocks, in_=blocks, compare_op=ALU.is_ge, fill=0.0, base=D - 1,
                                     pattern=[[D, NH], [0, D]], channel_multiplier=-1))
            quiet(pool.memset(picker[:, :], 0.0))
            for c in range(HC):
                quiet(pool.affine_select(out=picker[:, :], in_=picker[:, :], compare_op=ALU.not_equal, fill=1.0,
                                         base=-32 * c, pattern=[[-1, NE]], channel_multiplier=1))
            quiet(pool.memset(neg_half[:, :], -0.5))
            quiet(pool.iota(falling[:, 0, :], pattern=[[-1, NE]], base=NE, channel_multiplier=0,
                            allow_small_or_imprecise_dtypes=True))
            quiet(pool.iota(slot_base[:, 0, :], pattern=[[CAP, NE]], base=0, channel_multiplier=0,
                            allow_small_or_imprecise_dtypes=True))
            quiet(pool.iota(dest[:, :, :], pattern=[[1, TT], [NTOK, 2]], base=0, channel_multiplier=TT,
                            allow_small_or_imprecise_dtypes=True))
            for i in range(4):
                quiet(pool.memset(qa[i][:, :, :, MROW:STACK], 0.0))
                quiet(pool.memset(ka[i][:, :, :, MROW:STACK], 0.0))
                quiet(pool.memset(ka[i][:, :, :, MROW:MROW + 2], 1.0))
                quiet(pool.memset(ks[i][:, :, :], 0.0))
                quiet(pool.memset(va[i][:, :, :, D:32], 0.0))
                quiet(pool.memset(va[i][:, :, :, D:D + 1], 1.0))
            pool.memset(rest[:, :, :, :, :], 0.0).then_inc(pool_c, 1)
            pool.wait_ge(pool_c, 3)
            SET = q

            def hold(semaphore, count):
                need(pool, semaphore, count)
                if not isinstance(count, int):
                    pool.sem_inc(pool_waits, 1)

            def split(X, gx):
                i = gx % GB
                base = 6 * X
                hold(full["mT"], X - 3)
                hold(full["kT"], X - 3)
                pool.memset(qa[i][:, :, :, MROW:MROW + 2], 0.0)
                for n, (src, dst, first, second) in enumerate((
                        (qv[:, :, 0, :], qa[i], (0, 2, 3), (1, 2, 2)), (z[:, :, :], ka[i], (3, 1, 3), (0, 1, 2)))):
                    s = src.rearrange("p t (h d) -> p t h d", d=D)[:, :, HG * i:HG * i + HG, :]
                    d6 = dst[:, :, :, 0:MROW].rearrange("p t h (a d) -> p (t h) a d", d=D)
                    r = rest[:, n, :, :, :]
                    r3 = r.rearrange("p t h (a d) -> p (t h) a d", a=1)
                    lead = d6[:, :, first[0]:first[0] + first[1] * (first[2] - 1) + 1:first[1], :]
                    mid = d6[:, :, second[0]:second[0] + second[1] * (second[2] - 1) + 1:second[1], :]
                    last = d6[:, :, 5, :] if n == 0 else d6[:, :, 2, :]
                    st = stage[:, n, :, :, :]
                    pool.tensor_scalar(st, s, 1.0, 0.0, ALU.mult, ALU.add).then_inc(split_q, 1)
                    hold(split_q, base + 3 * n + 1)
                    st3 = st.rearrange("p t h (a d) -> p (t h) a d", a=1)
                    pool.tensor_scalar(lead, st3.broadcast_to([P, TT * HG, 3, D]), 1.0, 0.0, ALU.mult, ALU.add)
                    pool.tensor_tensor(r, s, st, ALU.subtract).then_inc(split_q, 1)
                    hold(split_q, base + 3 * n + 2)
                    pool.tensor_scalar(mid, r3.broadcast_to([P, TT * HG, 2, D]), 1.0, 0.0, ALU.mult, ALU.add)\
                        .then_inc(split_q, 1)
                    hold(split_q, base + 3 * n + 3)
                    ins = pool.tensor_tensor(last, r.rearrange("p t h d -> p (t h) d"), mid[:, :, 0, :],
                                             ALU.subtract)
                ins.then_inc(split_done, 1)

            def values(X, gx):
                i = gx % GB
                hold(av_part, TT * (X - 3))
                for tt in range(TT):
                    ins = pool.tensor_tensor(
                        va[i][:, tt, :, 0:D],
                        qv[:, tt, 1, :].rearrange("p (h d) -> p h d", d=D)[:, HG * i:HG * i + HG, :],
                        bv_row[:, :].rearrange("p (h d) -> p h d", d=D)[:, HG * i:HG * i + HG, :], ALU.add)
                ins.then_inc(v_done, 1)

            def maxima(X, gx):
                i = gx % GB
                m = neg_max[gx % 2]
                hold(full["qT"], X + 1)
                hold(max_done, TT * HG * (X + 1))
                pool.tensor_scalar(qa[i][:, :, :, MROW:MROW + 1], m[:, :, :, :], 1.0, 0.0, ALU.mult, ALU.add)\
                    .then_inc(split_m, 1)
                hold(split_m, SET + X + 1)
                pool.tensor_tensor(qa[i][:, :, :, MROW + 1:MROW + 2], m[:, :, :, :],
                                   qa[i][:, :, :, MROW:MROW + 1], ALU.subtract).then_inc(m_done, 1)

            def normalise(mv, ln, sem_q, i, out_of, src, ready):
                pool.tensor_scalar(ln[:, 0, :], mv[:, :, 1], 1.0, EPS, ALU.mult, ALU.add).then_inc(sem_q, 1)
                pool.tensor_scalar(ln[:, 2, :], mv[:, :, 0], -1.0, 0.0, ALU.mult, ALU.add).then_inc(sem_q, 1)
                hold(sem_q, 3 * i + 2)
                pool.tensor_tensor(ln[:, 1, :], ln[:, 0, :], neg_half[:, :], ALU.pow).then_inc(sem_q, 1)
                hold(sem_q, 3 * i + 3)
                for tt in range(TT):
                    ins = pool.tensor_scalar(out_of(tt), src(tt), ln[:, 2, tt:tt + 1], ln[:, 1, tt:tt + 1],
                                             ALU.add, ALU.mult)
                ins.then_inc(ready, 1)

            def dispatch(k, tiles):
                hold(route_done, k + 1)
                hold(blank_out, 16 * (1 + 2 * NB))
                for tt in tiles:
                    for c in range(2):
                        pool.indirect_dma_start(
                            out=rec_d, out_offset=bass.IndirectOffsetOnAxis(
                                ap=slot[:, c, tt, :].bitcast(U32), axis=0),
                            in_=rec[:, tt, c, :], in_offset=None, bounds_check=NE * CAP - 1,
                            oob_is_err=False).then_inc(rec_out, 16)

            def batch(b):
                for g in range(GB):
                    G = GB * b + g

                    def next_split(X, gx):
                        if live(X, NG):
                            if gx % GB == 0:
                                hold(done["qv"], 2 * (b + gx // GB + 1))
                            hold(z_done, b + gx // GB + 1)
                            split(X, gx)

                    def next_maxima():
                        if live(G + 1, NG):
                            maxima(G + 1, g + 1)

                    if g == 0:
                        if live(b - 2, NB):
                            dispatch(b - 2, (0,))
                        if live(b + 1, NB):
                            f = b + 1
                            hold(stat_a_done, f + 1)
                            hold(split_done, GB * f)
                            hold(full["zT"], f)
                            normalise(mv_a, ln_a, ln_q, f, lambda tt: z[:, tt, :], lambda tt: x_a[:, tt, :],
                                      z_done)
                        if live(b - 2, NB):
                            dispatch(b - 2, (1,))
                        next_maxima()
                        if live(b - 2, NB):
                            dispatch(b - 2, (2, 3))
                    elif g == 1:
                        if live(b - 1, NB):
                            k = b - 1
                            hold(stat_b_done, b)
                            hold(rec_out, 16 * 2 * TT * k)
                            normalise(mv_b, ln_b, ln2_q, k,
                                      lambda tt: rec[:, tt, :, 0:C],
                                      lambda tt: x2[:, tt:tt + 1, :].broadcast_to([P, 2, C]), y_norm)
                            pool.tensor_scalar(rec[:, :, :, C + 1].bitcast(I32), dest[:, :, :], 1.0, 0.0,
                                               ALU.mult, ALU.add).then_inc(dest_q, 1)
                            hold(dest_q, 2 * k + 1)
                            pool.tensor_scalar(dest[:, :, :], dest[:, :, :], 1.0, float(T), ALU.mult, ALU.add)\
                                .then_inc(dest_q, 1)
                            hold(dest_q, 2 * k + 2)
                        next_maxima()
                        next_split(G + 3, g + 3)
                    elif g == 2:
                        next_split(G + 3, g + 3)
                        next_maxima()
                    else:
                        next_split(G + 3, g + 3)
                        next_maxima()
                        next_split(G + 4, g + 4)
                    if live(G + 3, NG):
                        values(G + 3, g + 3)
                    if g == 2 and live(b, NB):
                        hold(xb_in, 16 * (b + 1))
                        hold(done["out"], b)
                        pool.tensor_tensor(x_bo[:, :, :], x_b[:, :, :],
                                           bo_row[:, :].rearrange("p (a c) -> p a c", a=1).broadcast_to([P, TT, C]),
                                           ALU.add).then_inc(xbo_done, 1)

            run_batches(pool, batch)
            dispatch(NB - 1, range(TT))

            def scatter(e, r):
                hold(y_done, e + 1)
                for n in range(TT):
                    pool.indirect_dma_start(
                        out=y_d, out_offset=bass.IndirectOffsetOnAxis(
                            ap=meta[r][:, n, 1:2].bitcast(U32), axis=0),
                        in_=y[r][:, n, :], in_offset=None, bounds_check=2 * NTOK - 1,
                        oob_is_err=False).then_inc(y_out[r], 16)

            def routing_of(e, r):
                hold(rl_in[r], 16 * (half(e) + 1))
                hold(y_out[r], 16 * TT * half(e))
                pool.tensor_copy(meta[r][:, :, :].bitcast(I32), rec_l[r][:, :, C:C + 2].bitcast(I32))\
                    .then_inc(meta_done, 1)
                hold(meta_done, e + 1)

            routing_of(0, 0)
            routing_of(1, 1)
            scatter(0, 0)
            scatter(1, 1)
            with pool.Fori(1, NE // 2) as i:
                for r in range(2):
                    routing_of(2 * i + r, r)
                    scatter(2 * i + r, r)


_INS = ['L0_attn_x', 'L0_attn_w_att_val', 'L0_attn_wv_w', 'L0_attn_wv_b', 'L0_attn_out_w', 'L0_attn_out_b',
        'L0_ffn_rw1', 'L0_ffn_rb1', 'L0_ffn_rw2', 'L0_ffn_rb2', 'L0_ffn_ew1', 'L0_ffn_eb1', 'L0_ffn_ew2',
        'L0_ffn_eb2']
_OUTS = [((NB, T, C), 'float32')]


def kernel(**inputs):
    import numpy as _np
    import concourse.bacc as _bacc
    from concourse import mybir as _mybir
    from concourse.bass_utils import run_bass_kernel_spmd as _run

    nc = _bacc.Bacc("TRN2", target_bir_lowering=False, num_devices=1)
    arrays, args = {}, []
    for name in _INS:
        a = _np.ascontiguousarray(inputs[name])
        arrays[f"in_{name}_dram"] = a
        args.append(nc.dram_tensor(f"in_{name}_dram", a.shape, _mybir.dt.from_np(a.dtype), kind="ExternalInput").ap())
    for i, (shape, dtype) in enumerate(_OUTS):
        dt = _mybir.dt.from_np(_np.dtype(dtype))
        args.append(nc.dram_tensor(f"out_{i}_dram", shape, dt, kind="ExternalOutput").ap())
    build(nc, *args)
    r = _run(nc, [arrays], core_ids=[0])
    got = tuple(r.results[0][f"out_{i}_dram"] for i in range(len(_OUTS)))
    return got[0]
```

```python
from contextlib import ExitStack

import concourse.bass as bass
from concourse import mybir

F32 = mybir.dt.float32
BF16 = mybir.dt.bfloat16
I32 = mybir.dt.int32
U32 = mybir.dt.uint32
ALU = mybir.AluOpType
ACT = mybir.ActivationFunctionType
AXIS = mybir.AxisListType

P = 128
NB, T, C = 8, 512, 128
NH, D = 16, 8
TT = T // P
HG = 4
GB = NH // HG
NG = NB * GB
STACK = 64
PARTS = 6
MROW = PARTS * D
NE, CAP, HID = 8, 512, 512
HC = HID // P
NTOK = NB * T
REC = C + 2
SCALE = float(D) ** -0.5
EPS = 1e-5
DROPPED = float(1 << 20)
SLOTS = 8
UNITS = HG * TT
BANK_PLAIN, BANK_ACC, BANK_SHARED = 3, 5, 6

SHARED = [
    (0, 0, "kT", 2, 0, 0), (0, 2, "qT", 2, 0, 0), (0, 2, "avT", -1, 0, 0), (0, 4, "oT", -1, 1, 0),
    (0, 5, "out", -1, 1, 0), (0, 6, "mT", 1, 0, 0), (0, 7, "zT", 1, 1, 0),
    (1, 0, "kT", 2, 0, 0), (1, 1, "qv", 1, 2, 0), (1, 2, "qT", 2, 0, 0), (1, 3, "avT", -1, 0, 0),
    (1, 4, "qv", 1, 2, 1), (1, 4, "yT", -1, 1, 0), (1, 5, "hid", -1, 4, 0), (1, 6, "mT", 1, 0, 0),
    (1, 7, "hid", -1, 4, 1),
    (2, 0, "kT", 2, 0, 0), (2, 0, "hid", -1, 4, 2), (2, 1, "hid", -1, 4, 3), (2, 2, "qT", 2, 0, 0),
    (2, 3, "avT", -1, 0, 0), (2, 4, "logT", -1, 1, 0), (2, 5, "logit", -1, 1, 0), (2, 6, "mT", 1, 0, 0),
    (3, 0, "kT", 2, 0, 0), (3, 2, "qT", 2, 0, 0), (3, 3, "avT", -1, 0, 0), (3, 4, "rank", -1, 1, 0),
    (3, 6, "mT", 1, 0, 0),
]
USES = ("kT", "qT", "mT", "avT", "oT", "zT", "qv", "out", "yT", "hid", "logT", "logit", "rank")


def live(i, n):
    return not isinstance(i, int) or 0 <= i < n


def need(eng, sem, count):
    if not isinstance(count, int) or count > 0:
        eng.wait_ge(sem, count)


def use_index(b, use):
    g, _, _, off, per, _ = use
    return b + off if per else GB * b + g + off


def use_exists(b, use):
    return live(use_index(b, use), NB if use[4] else NG)


def use_count(b, use):
    i = use_index(b, use)
    return i * use[4] + use[5] + 1 if use[4] else i + 1


def use_before(b, k):
    for back in range(4):
        for n in reversed(range(k if back == 0 else len(SHARED))):
            if use_exists(b - back, SHARED[n]) and use_bank(b - back, n) == use_bank(b, k):
                return SHARED[n][2], use_count(b - back, SHARED[n])
    return None


def use_bank(b, k):
    name, o = SHARED[k][2], SHARED[k][5]
    if isinstance(b, int) and (b, name) == (NB, "hid"):
        return o
    return BANK_SHARED + k % 2


def bank_named(name):
    return use_bank(0, [use[2] for use in SHARED].index(name))


def score_bank(n):
    return 1 if n == GB * UNITS - 1 else n % 3


def scores_before(b, n):
    m = n - 1
    while score_bank(m % (GB * UNITS)) != score_bank(n):
        m -= 1
    return GB * UNITS * b + m + 1


def plain_at(j):
    return (2 * j + UNITS // 2) % UNITS


def half(i):
    return i // 2


def run_batches(eng, body):
    body(-1)
    body(0)
    body(1)
    with eng.Fori(2, NB - 2) as b:
        body(b)
    body(NB - 2)
    body(NB - 1)
    body(NB)


def build(nc, x, w_att, wv_w, wv_b, out_w, out_b, rw1, rb1, rw2, rb2, ew1, eb1, ew2, eb2, out):
    rec_d = nc.dram_tensor("dispatched_rows", (NE * CAP, REC), F32).ap()
    y_d = nc.dram_tensor("expert_rows", (2 * NTOK, C), F32).ap()
    x_in = x.rearrange("b (p t) c -> b p t c", t=TT)
    rec_v = rec_d.rearrange("(e p n) r -> e p n r", p=P, n=TT)
    y_v = y_d.rearrange("(k b p t) c -> b p k t c", k=2, p=P, t=TT)
    out_v = out.rearrange("b (p t) c -> b p t c", t=TT)

    with ExitStack() as ctx:
        def sb(name, shape, dt=F32):
            return ctx.enter_context(nc.sbuf_tensor(name, shape, dt))

        def sem(name):
            return ctx.enter_context(nc.semaphore(name))

        ident = sb("ident", [P, P])
        identb = sb("identb", [P, P], BF16)
        before = sb("before", [P, P], BF16)
        onesb = sb("onesb", [P, P], BF16)
        w_small = sb("w_small", [P, D])
        w_qv = sb("w_qv", [P, 2, C])
        w_raw = sb("w_raw", [P, 2, C])
        w_out = sb("w_out", [P, C])
        bv_row = sb("bv_row", [P, C])
        bo_row = sb("bo_row", [P, C])
        b_raw = sb("b_raw", [NE * HC + HC, P])
        b_hid = sb("b_hid", [P, NE * HC + HC])
        rw1_s = sb("rw1_s", [P, HID])
        rw2_s = sb("rw2_s", [P, HC, 32])
        picker = sb("picker", [P, NE])
        rb2_row = sb("rb2_row", [P, NE])
        neg_half = sb("neg_half", [P, TT])
        falling = sb("falling", [P, 1, NE])
        slot_base = sb("slot_base", [P, 1, NE])
        x_a = sb("x_a", [P, TT, C])
        x_b = sb("x_b", [P, TT, C])
        x_bo = sb("x_bo", [P, TT, C])
        stat_a = sb("stat_a", [P, TT, 6])
        mv_a = sb("mv_a", [P, TT, 2])
        ln_a = sb("ln_a", [P, 3, TT])
        z = sb("z", [P, TT, C])
        zT = sb("zT", [P, T])
        qv = sb("qv", [P, TT, 2, C])
        stage = sb("stage", [P, 2, TT, HG, D], BF16)
        rest = sb("rest", [P, 2, TT, HG, D])
        qa = [sb(f"qa{i}", [P, TT, HG, STACK], BF16) for i in range(4)]
        ka = [sb(f"ka{i}", [P, TT, HG, STACK], BF16) for i in range(4)]
        va = [sb(f"va{i}", [P, TT, HG, 32]) for i in range(4)]
        ks = [sb(f"ks{i}", [P, HG, T], BF16) for i in range(4)]
        qs = [sb(f"qs{i}", [P, 2, T], BF16) for i in range(2)]
        qm = [sb(f"qm{i}", [P, 2, T], BF16) for i in range(2)]
        neg_max = [sb(f"neg_max{i}", [P, TT, HG, 1]) for i in range(2)]
        probs = sb("probs", [P, TT, HG, T])
        av = sb("av", [P, T])
        inv_sum = sb("inv_sum", [P, TT, HG, 1])
        o_tok = sb("o_tok", [P, TT, NH, D])
        oT = sb("oT", [P, T])
        x2 = sb("x2", [P, TT, C])
        x2_all = sb("x2_all", [P, NB, TT, C])
        stat_b = sb("stat_b", [P, TT, 6])
        mv_b = sb("mv_b", [P, TT, 2])
        ln_b = sb("ln_b", [P, 3, TT])
        rec = sb("rec", [P, TT, 2, REC])
        yT = sb("yT", [P, T])
        hid = sb("hid", [P, HC, T])
        logT = sb("logT", [P, T])
        logits = sb("logits", [P, TT, NE])
        tmp = sb("tmp", [P, TT, NE])
        top = sb("top", [P, 2, TT, 1])
        pick = sb("pick", [P, 2, TT, 1])
        chosen = sb("chosen", [P, 2, TT, NE])
        mask = sb("mask", [P, TT, NE], BF16)
        gap = sb("gap", [P, TT])
        e_gap = sb("e_gap", [P, TT])
        den = sb("den", [P, TT])
        taken = sb("taken", [P, NE])
        pos = sb("pos", [P, TT, NE])
        over = sb("over", [P, TT, NE])
        addr = sb("addr", [P, 1, TT, NE])
        slot_e = sb("slot_e", [P, 2, TT, NE])
        slot_f = sb("slot_f", [P, 2, TT, 1])
        slot = sb("slot", [P, 2, TT, 1], I32)
        dest = sb("dest", [P, TT, 2])
        blank = sb("blank", [P, 1, TT, REC])
        rec_l = [sb(f"rec_l{i}", [P, TT, REC]) for i in range(2)]
        w1 = [sb(f"w1_{i}", [P, HID]) for i in range(2)]
        w2 = [sb(f"w2_{i}", [P, HC, C]) for i in range(2)]
        b2 = [sb(f"b2_{i}", [P, 1, C]) for i in range(2)]
        meta = [sb(f"meta{i}", [P, TT, 2]) for i in range(2)]
        yb = [sb(f"yb{i}", [P, TT, C]) for i in range(2)]
        xT = [sb(f"xT{i}", [P, CAP]) for i in range(2)]
        hT = [sb(f"hT{i}", [P, HC, CAP]) for i in range(2)]
        y = [sb(f"y{i}", [P, TT, C]) for i in range(2)]
        f_y = [probs[:, i, 0:2, :].rearrange("p k (t c) -> p k t c", t=TT) for i in range(2)]
        f_s = [probs[:, i, 2, :].rearrange("p (t c) -> p t c", t=TT) for i in range(2)]
        f_o = [probs[:, i, 3, :].rearrange("p (t c) -> p t c", t=TT) for i in range(2)]

        ps = ctx.enter_context(nc.psum_tensor("ps", [P, 8, 512], F32))
        plain = [ps[:, BANK_PLAIN + i, :] for i in range(2)]
        acc = ps[:, BANK_ACC, :]

        att_in, raw_in, loaded = sem("att_in"), sem("raw_in"), sem("loaded")
        xa_in, xb_in, x2_out = sem("xa_in"), sem("xb_in"), sem("x2_out")
        blank_out, rec_out = sem("blank_out"), sem("rec_out")
        pool_c, dve_c, act_c, pe_c = sem("pool_c"), sem("dve_c"), sem("act_c"), sem("pe_c")
        pool_waits, dve_waits = sem("pool_waits"), sem("dve_waits")
        kT_done_2 = sem("kT_done_2")
        full = {n: sem(f"{n}_full") for n in USES}
        done = {n: sem(f"{n}_done") for n in USES}
        score_full, exp_done = sem("score_full"), sem("exp_done")
        plain_full, max_done = sem("plain_full"), sem("max_done")
        av_part, av_out = sem("av_part"), sem("av_out")
        split_k_done, split_done = sem("split_k_done"), sem("split_done")
        v_done, m_done = sem("v_done"), sem("m_done")
        stat_a_done, z_done = sem("stat_a_done"), sem("z_done")
        xbo_done, stat_b_done, y_norm = sem("xbo_done"), sem("stat_b_done"), sem("y_norm")
        gap_done, egap_done, mask_done, route_done = (sem("gap_done"), sem("egap_done"), sem("mask_done"),
                                                      sem("route_done"))
        setup_q, split_q, max_q, ln_q, ln2_q, dest_q = (sem("setup_q"), sem("split_q"), sem("max_q"),
                                                        sem("ln_q"), sem("ln2_q"), sem("dest_q"))
        st_q, st2_q, inv_q, route_q = sem("st_q"), sem("st2_q"), sem("inv_q"), sem("route_q")
        def two(name):
            return [sem(f"{name}{r}") for r in range(2)]

        w1_in, w2_in, rl_in, y_out = two("w1_in"), two("w2_in"), two("rl_in"), two("y_out")
        xT_full, xT_done = sem("xT_full"), sem("xT_done")
        h_full, h_act, h_dve = sem("h_full"), sem("h_act"), sem("h_dve")
        y_full, y_bias, y_done, meta_done = sem("y_full"), sem("y_bias"), sem("y_done"), sem("meta_done")
        f_in, done_out = two("f_in"), two("done_out")
        f_sum, f_done = sem("f_sum"), sem("f_done")

        block = ctx.enter_context(nc.Block())

        @block.sync
        def _(sp):
            sp.dma_start(x_a[:, :, :], x_in[0]).then_inc(xa_in, 16)
            sp.dma_start(w_small[:, :], w_att.rearrange("h d e -> (h d) e")).then_inc(att_in, 16)
            sp.dma_start(w_raw[:, 0, :], wv_w).then_inc(raw_in, 16)
            sp.dma_start(w_raw[:, 1, :], out_w).then_inc(raw_in, 16)
            sp.dma_start(b_raw[0:NE * HC, :], eb1.rearrange("e (c p) -> (e c) p", p=P)).then_inc(raw_in, 16)
            sp.dma_start(b_raw[NE * HC:NE * HC + HC, :], rb1.rearrange("(c p) -> c p", p=P)).then_inc(raw_in, 16)
            sp.wait_ge(pool_c, 1)
            sp.dma_start(rw2_s[:, :, 0:NE], rw2.rearrange("(c p) e -> p c e", p=P)).then_inc(loaded, 16)

            def weights_2(e, r):
                sp.dma_start(w2[r][:, :, :], ew2[e].rearrange("(c p) n -> p c n", p=P)).then_inc(w2_in[r], 16)
                sp.dma_start(b2[r][:, :, :], eb2[bass.ds(e, 1), :].rearrange("(a b) c -> a b c", a=1)
                             .broadcast_to([P, 1, C])).then_inc(w2_in[r], 16)

            def prepare():
                sp.dma_start(rec_d.rearrange("(p e n) r -> p e n r", p=P, n=TT),
                             blank[:, :, :, :].broadcast_to([P, NE, TT, REC])).then_inc(blank_out, 16)
                for k in range(2):
                    for b in range(NB):
                        sp.dma_start(y_v[b][:, k, :, :], blank[:, 0, :, 0:C]).then_inc(blank_out, 16)
                for r in range(2):
                    sp.dma_start(w1[r][:, :], ew1[r]).then_inc(w1_in[r], 16)
                    weights_2(r, r)

            def batch(b):
                f, k = b + 2, b - 1
                if live(b, NB):
                    need(sp, xbo_done, b)
                    sp.dma_start(x_b[:, :, :], x_in[b]).then_inc(xb_in, 16)
                if live(f, NB):
                    need(sp, z_done, TT * f)
                    sp.dma_start(x_a[:, :, :], x_in[f]).then_inc(xa_in, 16)
                if isinstance(b, int) and b == 0:
                    prepare()
                if live(k, NB):
                    sp.wait_ge(done["out"], k + 1)
                    sp.dma_start(x2_all[:, bass.ds(k, 1), :, :], x2[:, :, :]).then_inc(x2_out, 16)

            run_batches(sp, batch)

            def rows(e, r):
                need(sp, xT_full, e - 1)
                need(sp, meta_done, e - 1)
                sp.dma_start(rec_l[r][:, :, :], rec_v[e]).then_inc(rl_in[r], 16)

            def expert(e, r):
                rows(e, r)
                need(sp, h_full, HC * (e - 1))
                sp.dma_start(w1[r][:, :], ew1[e]).then_inc(w1_in[r], 16)
                need(sp, y_bias, e - 1)
                weights_2(e, r)

            sp.wait_ge(rec_out, 16 * 2 * TT * NB)
            rows(0, 0)
            rows(1, 1)
            with sp.Fori(1, NE // 2) as i:
                expert(2 * i, 0)
                expert(2 * i + 1, 1)

            def finish(c, r):
                need(sp, f_sum, c - 1)
                sp.dma_start(f_y[r][:, :, :, :], y_v[c]).then_inc(f_in[r], 16)

            for r in range(2):
                sp.wait_ge(y_out[r], 16 * TT * NE // 2)
            finish(0, 0)
            finish(1, 1)
            with sp.Fori(1, NB // 2) as i:
                finish(2 * i, 0)
                finish(2 * i + 1, 1)
            for r in range(2):
                sp.wait_ge(done_out[r], 16 * NB // 2)

        @block.tensor
        def _(pe):
            pe.wait_ge(raw_in, 16 * 4)
            pe.wait_ge(pool_c, 1)
            pe.transpose(ps[:, 0, 0:P], w_raw[:, 0, :], ident[:, :])
            pe.transpose(ps[:, 0, P:2 * P], w_raw[:, 1, :], ident[:, :])
            pe.transpose(ps[:, 0, 2 * P:2 * P + NE * HC + HC], b_raw[:, :],
                         ident[0:NE * HC + HC, 0:NE * HC + HC]).then_inc(pe_c, 1)
            pe.wait_ge(act_c, 1)
            pe.wait_ge(pool_c, 2)
            pe.wait_ge(loaded, 16 * 5)
            pe.wait_ge(dve_c, 1)

            def scores(b, G, g, j):
                st, pair = j // 2, j % 2
                if j == 0:
                    need(pe, done["mT"], G + 1)
                for i in range(2):
                    n = UNITS * g + 2 * j + i
                    need(pe, exp_done, scores_before(b, n))
                    pe.matmul(ps[:, score_bank(n), :], ks[g][:, 2 * pair + i, st * P:(st + 1) * P],
                              qm[g % 2][:, pair, :], start=True, stop=True).then_inc(score_full, 1)

            def values(G, g, st):
                if st == 0:
                    need(pe, av_out, G)
                    need(pe, v_done, G + 1)
                need(pe, exp_done, UNITS * G + HG * (st + 1))
                for h in range(HG):
                    mm = pe.matmul(acc[32 * h:32 * h + 32, :], va[g][:, st, h, :], probs[:, st, h, :],
                                   start=(st == 0), stop=(st == TT - 1))
                mm.then_inc(av_part, 1)

            def plain_scores(X, gx, u):
                tt, h = u // HG, u % HG
                if u == 0:
                    need(pe, done["kT"], X + 1)
                    need(pe, kT_done_2, X + 1)
                    need(pe, done["qT"], X + 1)
                need(pe, max_done, TT * HG * X + u - 1)
                pe.matmul(plain[u % 2], qs[gx % 2][:, h // 2, tt * P:(tt + 1) * P],
                          ks[gx % 4][:, h, :], start=True, stop=True).then_inc(plain_full, 1)

            def stack_transposes(shared, src):
                for pair in range(2):
                    for tt in range(TT):
                        n = pair * TT + tt
                        mm = pe.transpose(shared.bitcast(BF16)[:, n * P:(n + 1) * P],
                                          src[:, tt, 2 * pair:2 * pair + 2, :].rearrange("p h c -> p (h c)"),
                                          identb[:, :])
                return mm

            def token_transposes(shared, tile):
                for tt in range(TT):
                    mm = pe.transpose(shared[:, tt * P:(tt + 1) * P], tile(tt), ident[:, :])
                return mm

            def shared_use(b, k):
                g, _, name, off, _, o = SHARED[k]
                i = use_index(b, SHARED[k])
                shared = ps[:, use_bank(b, k), :]
                prior = use_before(b, k)
                if prior:
                    need(pe, done[prior[0]], prior[1])
                    if prior[0] == "kT":
                        need(pe, kT_done_2, prior[1])
                if name == "kT":
                    need(pe, split_k_done, i + 1)
                    mm = stack_transposes(shared, ka[(g + off) % 4])
                elif name == "qT":
                    need(pe, split_done, i + 1)
                    mm = stack_transposes(shared, qa[(g + off) % 4])
                elif name == "mT":
                    need(pe, m_done, i + 1)
                    mm = stack_transposes(shared, qa[(g + off) % 4])
                elif name == "avT":
                    need(pe, av_out, i + 1)
                    mm = token_transposes(shared, lambda tt: av[:, tt * P:(tt + 1) * P])
                elif name == "oT":
                    need(pe, done["avT"], GB * (i + 1))
                    mm = token_transposes(shared, lambda tt: o_tok[:, tt, :, :].rearrange("p h d -> p (h d)"))
                elif name == "zT":
                    for tt in range(TT):
                        need(pe, z_done, TT * i + tt + 1)
                        mm = pe.transpose(shared[:, tt * P:(tt + 1) * P], z[:, tt, :], ident[:, :])
                elif name == "yT":
                    for tt in range(TT):
                        need(pe, y_norm, TT * i + tt + 1)
                        mm = pe.transpose(shared[:, tt * P:(tt + 1) * P], rec[:, tt, 0, 0:C], ident[:, :])
                elif name == "qv":
                    need(pe, done["zT"], i + 1)
                    for n in range(2):
                        tt = 2 * o + n
                        mm = pe.matmul(shared[:, n * 2 * C:(n + 1) * 2 * C], zT[:, tt * P:(tt + 1) * P],
                                       w_qv[:, :, :].rearrange("p a c -> p (a c)"), start=True, stop=True)
                elif name == "out":
                    need(pe, done["oT"], i + 1)
                    for tt in range(TT):
                        mm = pe.matmul(shared[:, tt * C:(tt + 1) * C], oT[:, tt * P:(tt + 1) * P], w_out[:, :],
                                       start=True, stop=True)
                elif name == "hid":
                    need(pe, done["yT"], i + 1)
                    mm = pe.matmul(shared, rw1_s[:, o * P:(o + 1) * P], yT[:, :], start=True, stop=True)
                elif name == "logT":
                    pe.wait_ge(pool_c, 3)
                    need(pe, done["hid"], HC * (i + 1))
                    for c in range(HC):
                        mm = pe.matmul(shared[32 * c:32 * c + 32, :], rw2_s[:, c, :], hid[:, c, :],
                                       start=True, stop=True)
                elif name == "logit":
                    need(pe, done["logT"], i + 1)
                    for tt in range(TT):
                        mm = pe.matmul(shared[:, tt * NE:(tt + 1) * NE], logT[:, tt * P:(tt + 1) * P],
                                       picker[:, :], start=True, stop=True)
                elif name == "rank":
                    need(pe, mask_done, i + 1)
                    for n, w in enumerate((before, onesb)):
                        for tt in range(TT):
                            mm = pe.matmul(shared[:, n * NE:(n + 1) * NE], w[:, :], mask[:, tt, :],
                                           start=(tt == 0), stop=(tt == TT - 1))
                mm.then_inc(full[name], 1)

            def batch(b):
                for g in range(GB):
                    G = GB * b + g
                    for j in range(SLOTS):
                        if live(G, NG):
                            scores(b, G, g, j)
                        X, gx = (G + 1, g + 1) if j < 4 else (G + 2, g + 2)
                        uses = [k for k, use in enumerate(SHARED) if use[0:2] == (g, j) and use_exists(b, use)]
                        if live(X, NG):
                            plain_scores(X, gx, plain_at(j))
                        if j == 1 and live(G - 1, NG):
                            values(G - 1, (g - 1) % 4, 3)
                        elif j % 2 and j > 1 and live(G, NG):
                            values(G, g, (j - 3) // 2)
                        elif j % 2 == 0:
                            for k in uses:
                                shared_use(b, k)
                        if live(X, NG):
                            plain_scores(X, gx, plain_at(j) + 1)
                        if j % 2:
                            for k in uses:
                                shared_use(b, k)

            run_batches(pe, batch)

            def rows_T(e, r):
                pe.wait_ge(rl_in[r], 16 * (half(e) + 1))
                need(pe, xT_done, e - 1)
                for n in range(TT):
                    mm = pe.transpose(ps[:, r, n * P:(n + 1) * P], rec_l[r][:, n, 0:C], ident[:, :])
                mm.then_inc(xT_full, 1)

            def first(e, r, chunks):
                pe.wait_ge(w1_in[r], 16 * (half(e) + 1))
                pe.wait_ge(xT_done, e + 1)
                for c in chunks:
                    need(pe, h_act if c < 2 else h_dve, 2 * (e - 1) + c % 2 + 1)
                    pe.matmul(ps[:, 2 + c, :], w1[r][:, c * P:(c + 1) * P], xT[r][:, :],
                              start=True, stop=True).then_inc(h_full, 1)

            def second(e, r):
                pe.wait_ge(w2_in[r], 32 * (half(e) + 1))
                pe.wait_ge(h_act, 2 * (e + 1))
                pe.wait_ge(h_dve, 2 * (e + 1))
                need(pe, y_bias, e - 1)
                for n in range(TT):
                    for c in range(HC):
                        mm = pe.matmul(ps[:, 6 + r, n * C:(n + 1) * C], hT[r][:, c, n * P:(n + 1) * P],
                                       w2[r][:, c, :], start=(c == 0), stop=(c == HC - 1))
                mm.then_inc(y_full, 1)

            def expert(e, r, last=False):
                first(e, r, (0, 1))
                second(e - 1, 1 - r)
                if not last:
                    rows_T(e + 1, 1 - r)
                first(e, r, (2, 3))

            pe.wait_ge(exp_done, UNITS * NG)
            pe.wait_ge(max_done, TT * HG * NG)
            pe.wait_ge(av_out, NG)
            pe.wait_ge(done["rank"], NB)
            rows_T(0, 0)
            first(0, 0, (0, 1))
            rows_T(1, 1)
            first(0, 0, (2, 3))
            expert(1, 1)
            with pe.Fori(1, NE // 2 - 1) as i:
                expert(2 * i, 0)
                expert(2 * i + 1, 1)
            expert(NE - 2, 0)
            expert(NE - 1, 1, last=True)
            second(NE - 1, 1)

        @block.scalar
        def _(act):
            def load(dst, src):
                act.dma_start(dst, src).then_inc(loaded, 16)

            load(bv_row[:, :], wv_b.rearrange("(a c) -> a c", a=1).broadcast_to([P, C]))
            load(bo_row[:, :], out_b.rearrange("(a c) -> a c", a=1).broadcast_to([P, C]))
            load(rw1_s[:, :], rw1)
            load(rb2_row[:, :], rb2.rearrange("(a c) -> a c", a=1).broadcast_to([P, NE]))
            act.wait_ge(pool_c, 1)
            act.activation(identb[:, :], ident[:, :], ACT.Copy)
            act.wait_ge(pe_c, 1)
            act.activation(w_qv[:, 1, :], ps[:, 0, 0:P], ACT.Copy)
            act.activation(w_out[:, :], ps[:, 0, P:2 * P], ACT.Copy)
            act.activation(b_hid[:, :], ps[:, 0, 2 * P:2 * P + NE * HC + HC], ACT.Copy).then_inc(act_c, 1)
            act.wait_ge(act_c, 1)

            def exps(G, g, j):
                st, pair = j // 2, j % 2
                need(act, av_part, TT * (G - 1) + st + 1)
                for i in range(2):
                    act.wait_ge(score_full, UNITS * G + 2 * j + i + 1)
                    act.activation(probs[:, st, 2 * pair + i, :], ps[:, score_bank(UNITS * g + 2 * j + i), :],
                                   ACT.Exp, scale=SCALE).then_inc(exp_done, 1)

            def read_out(b, k):
                use = SHARED[k]
                g, _, name, off, _, o = use
                i = use_index(b, use)
                dst, func, bias = None, ACT.Copy, 0.0
                src = ps[:, use_bank(b, k), :]
                if name == "kT":
                    dst = ks[(g + off) % 4][0:STACK, 0:HG:2, :]
                    src = src.bitcast(BF16)[0:STACK, :].rearrange("p (a t) -> p a t", a=2)
                    act.wait_ge(dve_c, 2)
                    need(act, score_full, UNITS * (i - 3))
                elif name == "qT":
                    dst, src = qs[(g + off) % 2][:, :, :].rearrange("p a t -> p (a t)"), src.bitcast(BF16)
                    need(act, plain_full, TT * HG * (i - 1))
                elif name == "mT":
                    dst, src = qm[(g + off) % 2][:, :, :].rearrange("p a t -> p (a t)"), src.bitcast(BF16)
                    need(act, score_full, UNITS * (i - 1))
                elif name == "oT":
                    dst = oT[:, :]
                    need(act, full["out"], i)
                elif name == "zT":
                    dst = zT[:, :]
                    need(act, full["qv"], 2 * i)
                elif name == "yT":
                    dst = yT[:, :]
                    need(act, full["hid"], HC * i)
                elif name == "qv":
                    dst = qv[:, 2 * o:2 * o + 2, :, :].rearrange("p t a c -> p (t a c)")
                    need(act, split_done, GB * i)
                    need(act, v_done, GB * i)
                elif name == "hid":
                    dst, func, bias = hid[:, o, :], ACT.Relu, b_hid[:, NE * HC + o:NE * HC + o + 1]
                    need(act, full["logT"], i)
                elif name == "logT":
                    dst = logT[:, :]
                    need(act, full["logit"], i)
                else:
                    return
                act.wait_ge(full[name], use_count(b, use))
                act.activation(dst, src, func, bias=bias).then_inc(done[name], 1)

            def batch(b):
                for g in range(GB):
                    G = GB * b + g
                    for j in range(SLOTS):
                        if live(G, NG):
                            exps(G, g, j)
                        if j == 1 and live(G - 1, NG):
                            act.wait_ge(av_part, TT * G)
                            need(act, full["avT"], G - 1)
                            act.activation(av[:, :], acc, ACT.Copy).then_inc(av_out, 1)
                        for k, use in enumerate(SHARED):
                            if use[0:2] == (g, j) and use_exists(b, use):
                                read_out(b, k)
                        if (g, j) == (3, 2) and live(b - 1, NB):
                            act.wait_ge(gap_done, b)
                            act.activation(e_gap[:, :], gap[:, :], ACT.Exp).then_inc(egap_done, 1)

            run_batches(act, batch)

            def expert(e, r):
                act.wait_ge(xT_full, e + 1)
                act.activation(xT[r][:, :], ps[:, r, :], ACT.Copy).then_inc(xT_done, 1)
                need(act, y_full, e - 1)
                for c in range(2):
                    act.wait_ge(h_full, HC * e + c + 1)
                    act.activation(hT[r][:, c, :], ps[:, 2 + c, :], ACT.Relu,
                                   bias=b_hid[:, bass.ds(HC * e + c, 1)]).then_inc(h_act, 1)

            expert(0, 0)
            expert(1, 1)
            with act.Fori(1, NE // 2) as i:
                expert(2 * i, 0)
                expert(2 * i + 1, 1)

            def store(c, r):
                act.wait_ge(f_done, c + 1)
                act.dma_start(out_v[c], f_o[r][:, :, :]).then_inc(done_out[r], 16)

            with act.Fori(0, NB // 2) as i:
                store(2 * i, 0)
                store(2 * i + 1, 1)

        @block.vector
        def _(v):
            v.memset(taken[:, :], 0.0)
            for i in range(4):
                v.memset(qa[i][:, :, :, MROW:STACK], 0.0)
                v.memset(ka[i][:, :, :, MROW + 2:STACK], 0.0)
                ins = v.memset(ka[i][:, :, :, MROW:MROW + 2], 1.0)
            ins.then_inc(dve_c, 1)

            def fill_keys_and_values():
                for i in range(4):
                    v.memset(ks[i][:, :, :], 0.0)
                    v.memset(va[i][:, :, :, D + 1:32], 0.0)
                    ins = v.memset(va[i][:, :, :, D:D + 1], 1.0)
                ins.then_inc(dve_c, 1)

            def statistics(part, src, stat, mv, q, i, ready):
                if part < 2:
                    for tt in (2 * part, 2 * part + 1):
                        v.bn_stats(stat[:, tt, :], src[:, tt, :]).then_inc(q, 1)
                    return
                for tt in range(TT):
                    v.wait_ge(q, TT * i + tt + 1)
                    if not isinstance(i, int):
                        v.sem_inc(dve_waits, 1)
                    a = v.bn_aggr(mv[:, tt, :], stat[:, tt, :])
                a.then_inc(ready, 1)

            def read_out(b, k):
                use = SHARED[k]
                g, _, name, off, _, _ = use
                i = use_index(b, use)
                shared = ps[:, use_bank(b, k), :]
                shared_b = shared.bitcast(BF16)
                if name == "kT":
                    need(v, score_full, UNITS * (i - 3))
                    v.wait_ge(full["kT"], i + 1)
                    v.tensor_copy(ks[(g + off) % 4][STACK:P, 1:HG:2, :],
                                  shared_b[STACK:P, :].rearrange("p (a t) -> p a t", a=2)).then_inc(kT_done_2, 1)
                elif name == "avT":
                    t4 = shared.rearrange("p (t h c) -> p t h c", t=TT, h=HG)
                    v.wait_ge(full["avT"], i + 1)
                    v.reciprocal(inv_sum[:, :, :, :], t4[:, :, :, D:D + 1]).then_inc(inv_q, 1)
                    v.wait_ge(inv_q, i + 1)
                    if (g + off) % GB == 0:
                        need(v, full["oT"], b + (g + off) // GB)
                    h0 = HG * ((g + off) % GB)
                    v.tensor_tensor(o_tok[:, :, h0:h0 + HG, :], t4[:, :, :, 0:D],
                                    inv_sum[:, :, :, :].broadcast_to([P, TT, HG, D]), ALU.mult)\
                     .then_inc(done["avT"], 1)
                elif name == "out":
                    v.wait_ge(xbo_done, i + 1)
                    need(v, x2_out, 16 * i)
                    need(v, y_norm, TT * i)
                    v.wait_ge(full["out"], i + 1)
                    v.tensor_tensor(x2[:, :, :].rearrange("p t c -> p (t c)"), shared,
                                    x_bo[:, :, :].rearrange("p t c -> p (t c)"), ALU.add)\
                     .then_inc(done["out"], 1)

            CHAIN = 24

            def route(i, h):
                n = CHAIN * i + (0, 0, 0, 1, 2, 3, 4, 5, 6, 7, 8, 9, 10, 11, 11, 12, 13, 15, 17, 19, 21, 23)[h]

                def step(ins):
                    nonlocal n
                    n += 1
                    ins.then_inc(route_q, 1)

                def last():
                    v.wait_ge(route_q, n)

                def largest(k):
                    step(v.tensor_reduce(top[:, k, :, :], logits[:, :, :], AXIS.X, ALU.max))

                def at_largest(k):
                    step(v.tensor_tensor(tmp[:, :, :], logits[:, :, :], top[:, k, :, :].broadcast_to([P, TT, NE]),
                                         ALU.is_equal))

                def numbered(k):
                    step(v.tensor_tensor(tmp[:, :, :], tmp[:, :, :], falling[:, :, :].broadcast_to([P, TT, NE]),
                                         ALU.mult))

                def first_place(k):
                    step(v.tensor_reduce(pick[:, k, :, :], tmp[:, :, :], AXIS.X, ALU.max))

                def one_hot(k):
                    step(v.tensor_tensor(chosen[:, k, :, :], falling[:, :, :].broadcast_to([P, TT, NE]),
                                         pick[:, k, :, :].broadcast_to([P, TT, NE]), ALU.is_equal))

                if h == 1:
                    v.wait_ge(pool_c, 3)
                    v.wait_ge(full["logit"], i + 1)
                    need(v, egap_done, i)
                    v.tensor_tensor(logits[:, :, :],
                                    ps[:, bank_named("logit"), 0:TT * NE].rearrange("p (t e) -> p t e", t=TT),
                                    rb2_row[:, :].rearrange("p (a e) -> p a e", a=1).broadcast_to([P, TT, NE]),
                                    ALU.add).then_inc(done["logit"], 1)
                elif h == 2:
                    v.wait_ge(done["logit"], i + 1)
                    largest(0)
                elif h in (3, 9):
                    last()
                    if h == 9:
                        v.tensor_tensor(gap[:, :], top[:, 1, :, 0], top[:, 0, :, 0], ALU.subtract)\
                         .then_inc(gap_done, 1)
                    at_largest(h // 9)
                elif h in (4, 10):
                    last()
                    numbered(h // 10)
                elif h in (5, 11):
                    last()
                    first_place(h // 11)
                elif h in (6, 12):
                    last()
                    one_hot(h // 12)
                elif h == 7:
                    last()
                    step(v.scalar_tensor_tensor(out=logits[:, :, :], in0=chosen[:, 0, :, :], scalar=-3.0e38,
                                                in1=logits[:, :, :], op0=ALU.mult, op1=ALU.add))
                elif h == 8:
                    last()
                    largest(1)
                elif h == 13:
                    last()
                    need(v, full["rank"], i)
                    v.tensor_tensor(mask[:, :, :], chosen[:, 0, :, :], chosen[:, 1, :, :], ALU.add)\
                     .then_inc(mask_done, 1)
                elif h == 14:
                    v.wait_ge(egap_done, i + 1)
                    step(v.tensor_scalar(den[:, :], e_gap[:, :], 1.0, None, ALU.add))
                elif h == 15:
                    last()
                    step(v.reciprocal(den[:, :], den[:, :]))
                elif h == 16:
                    last()
                    need(v, rec_out, 16 * 2 * TT * i)
                    step(v.tensor_copy(rec[:, :, 0, C], den[:, :]))
                    step(v.tensor_tensor(rec[:, :, 1, C], e_gap[:, :], den[:, :], ALU.mult))
                    v.wait_ge(full["rank"], i + 1)
                    v.tensor_tensor(pos[:, 0, :], ps[:, bank_named("rank"), 0:NE], taken[:, :], ALU.add)
                    v.tensor_tensor(taken[:, :], ps[:, bank_named("rank"), NE:2 * NE], taken[:, :], ALU.add)\
                     .then_inc(done["rank"], 1)
                elif h == 17:
                    v.wait_ge(done["rank"], i + 1)
                    step(v.tensor_tensor(pos[:, 1, :], pos[:, 0, :], mask[:, 0, :], ALU.add))
                    last()
                    step(v.tensor_tensor(pos[:, 2, :], pos[:, 1, :], mask[:, 1, :], ALU.add))
                elif h == 18:
                    last()
                    step(v.tensor_tensor(pos[:, 3, :], pos[:, 2, :], mask[:, 2, :], ALU.add))
                    last()
                    step(v.tensor_scalar(over[:, :, :], pos[:, :, :], float(CAP), DROPPED, ALU.is_ge, ALU.mult))
                elif h == 19:
                    last()
                    step(v.tensor_tensor(over[:, :, :], over[:, :, :], pos[:, :, :], ALU.add))
                    last()
                    step(v.tensor_tensor(addr[:, 0, :, :], over[:, :, :],
                                         slot_base[:, :, :].broadcast_to([P, TT, NE]), ALU.add))
                elif h == 20:
                    last()
                    for k in range(2):
                        step(v.tensor_tensor(slot_e[:, k, :, :], chosen[:, k, :, :], addr[:, 0, :, :], ALU.mult))
                elif h == 21:
                    last()
                    step(v.tensor_reduce(slot_f[:, :, :, :], slot_e[:, :, :, :], AXIS.X, ALU.add))
                    last()
                    v.tensor_copy(slot[:, :, :, :], slot_f[:, :, :, :]).then_inc(route_done, 1)

            def maximum(X, gx, u):
                if u == 0:
                    need(v, m_done, X - 1)
                v.wait_ge(plain_full, TT * HG * X + u + 1)
                v.tensor_reduce(neg_max[gx % 2][:, u // HG, u % HG, :], plain[u % 2], AXIS.X,
                                ALU.max, negate=True).then_inc(max_done, 1)

            def side_work(b, g, h):
                if g == 1 and live(b + 2, NB) and 4 <= h < 7:
                    if h == 4:
                        v.wait_ge(xa_in, 16 * (b + 3))
                        v.wait_ge(z_done, TT * (b + 2))
                    statistics(h - 4, x_a, stat_a, mv_a, st_q, b + 2, stat_a_done)
                if g == 0 and live(b - 1, NB) and 12 <= h < 15:
                    if h == 12:
                        v.wait_ge(done["out"], b)
                    statistics(h - 12, x2, stat_b, mv_b, st2_q, b - 1, stat_b_done)
                if (g, h) >= (2, 11) and live(b - 1, NB):
                    route(b - 1, h - 10 if g == 2 else h + 6)

            def batch(b):
                for g in range(GB):
                    G = GB * b + g
                    for j in range(SLOTS):
                        X, gx = (G + 1, g + 1) if j < 4 else (G + 2, g + 2)
                        if live(X, NG):
                            maximum(X, gx, plain_at(j))
                        uses = [k for k, use in enumerate(SHARED) if use[0:2] == (g, j) and use_exists(b, use)]
                        if j % 2 == 0:
                            for k in uses:
                                read_out(b, k)
                        side_work(b, g, 2 * j)
                        if live(X, NG):
                            maximum(X, gx, plain_at(j) + 1)
                        side_work(b, g, 2 * j + 1)
                        if j % 2:
                            for k in uses:
                                read_out(b, k)

            v.wait_ge(xa_in, 16)
            for part in range(3):
                statistics(part, x_a, stat_a, mv_a, st_q, 0, stat_a_done)
            fill_keys_and_values()
            v.wait_ge(dve_c, 2)
            v.wait_ge(loaded, 16 * 5)
            run_batches(v, batch)

            def routing_of(e, r):
                v.wait_ge(rl_in[r], 16 * (half(e) + 1))
                need(v, y_out[r], 16 * TT * half(e))
                v.tensor_copy(meta[r][:, :, :].bitcast(I32), rec_l[r][:, :, C:C + 2].bitcast(I32))\
                 .then_inc(meta_done, 1)

            def expert(e, r):
                routing_of(e, r)
                need(v, y_full, e - 1)
                for c in range(2, HC):
                    v.wait_ge(h_full, HC * e + c + 1)
                    v.tensor_scalar(hT[r][:, c, :], ps[:, 2 + c, :], b_hid[:, bass.ds(HC * e + c, 1)], 0.0,
                                    ALU.add, ALU.max).then_inc(h_dve, 1)

            def weigh(e, r):
                need(v, y_out[r], 16 * TT * half(e))
                v.wait_ge(meta_done, e + 1)
                v.wait_ge(y_full, e + 1)
                v.tensor_tensor(yb[r][:, :, :], ps[:, 6 + r, :].rearrange("p (t c) -> p t c", t=TT),
                                b2[r][:, :, :].broadcast_to([P, TT, C]), ALU.add).then_inc(y_bias, 1)
                v.wait_ge(y_bias, e + 1)
                for n in range(TT):
                    v.tensor_tensor(y[r][:, n, :], yb[r][:, n, :],
                                    meta[r][:, n, 0:1].broadcast_to([P, C]), ALU.mult).then_inc(y_done, 1)

            expert(0, 0)
            weigh(0, 0)
            expert(1, 1)
            with v.Fori(1, NE // 2) as i:
                for r in range(2):
                    weigh(2 * i + r - 1, 1 - r)
                    expert(2 * i + r, r)
            weigh(NE - 1, 1)

            v.wait_ge(x2_out, 16 * NB)

            def finish(c, r):
                v.wait_ge(f_in[r], 16 * (half(c) + 1))
                v.tensor_tensor(f_s[r][:, :, :], f_y[r][:, 0, :, :], f_y[r][:, 1, :, :], ALU.add).then_inc(f_sum, 1)
                v.wait_ge(f_sum, c + 1)
                need(v, done_out[r], 16 * half(c))
                v.tensor_tensor(f_o[r][:, :, :], x2_all[:, bass.ds(c, 1), :, :].rearrange("p a t c -> p (a t) c"),
                                f_s[r][:, :, :], ALU.add).then_inc(f_done, 1)

            finish(0, 0)
            finish(1, 1)
            with v.Fori(1, NB // 2) as i:
                finish(2 * i, 0)
                finish(2 * i + 1, 1)

        @block.gpsimd
        def _(pool):
            steps = 0

            def finished(ins):
                nonlocal steps
                steps += 1
                ins.then_inc(setup_q, 1)
                pool.wait_ge(setup_q, steps)

            finished(pool.memset(ident[:, :], 0.0))
            finished(pool.affine_select(out=ident[:, :], in_=ident[:, :], compare_op=ALU.not_equal, fill=1.0, base=0,
                                     pattern=[[-1, P]], channel_multiplier=1))
            finished(pool.memset(rw2_s[:, :, :], 0.0))
            finished(pool.memset(blank[:, :, :, :], 0.0))
            pool.memset(blank[:, :, :, C + 1], 1.0e9).then_inc(pool_c, 1)
            blocks = w_qv[:, 0, :].rearrange("p (h e) -> p h e", h=NH)
            pool.wait_ge(att_in, 16)
            finished(pool.tensor_copy(blocks, w_small[:, :].rearrange("p (a e) -> p a e", a=1)
                                      .broadcast_to([P, NH, D])))
            finished(pool.affine_select(out=blocks, in_=blocks, compare_op=ALU.is_ge, fill=0.0, base=0,
                                     pattern=[[-D, NH], [0, D]], channel_multiplier=1))
            finished(pool.affine_select(out=blocks, in_=blocks, compare_op=ALU.is_ge, fill=0.0, base=D - 1,
                                     pattern=[[D, NH], [0, D]], channel_multiplier=-1))
            pool.memset(neg_half[:, :], -0.5).then_inc(pool_c, 1)
            pool.wait_ge(pool_c, 2)
            pool.wait_ge(dve_c, 1)

            def router_constants():
                finished(pool.memset(onesb[:, :], 1.0))
                pool.affine_select(out=before[:, :], in_=onesb[:, :], compare_op=ALU.is_gt, fill=0.0, base=0,
                                   pattern=[[1, P]], channel_multiplier=-1)
                finished(pool.memset(picker[:, :], 0.0))
                for c in range(HC):
                    finished(pool.affine_select(out=picker[:, :], in_=picker[:, :], compare_op=ALU.not_equal,
                                                fill=1.0, base=-32 * c, pattern=[[-1, NE]], channel_multiplier=1))
                pool.iota(falling[:, 0, :], pattern=[[-1, NE]], base=NE, channel_multiplier=0,
                          allow_small_or_imprecise_dtypes=True)
                pool.iota(slot_base[:, 0, :], pattern=[[CAP, NE]], base=0, channel_multiplier=0,
                          allow_small_or_imprecise_dtypes=True)
                pool.iota(dest[:, :, :], pattern=[[1, TT], [NTOK, 2]], base=0, channel_multiplier=TT,
                          allow_small_or_imprecise_dtypes=True).then_inc(pool_c, 1)
                pool.wait_ge(pool_c, 3)

            def hold(semaphore, count):
                need(pool, semaphore, count)
                if not isinstance(count, int):
                    pool.sem_inc(pool_waits, 1)

            def split(X, gx, batches):
                i = gx % GB
                hold(full["mT"], X - 3)
                hold(full["kT"], X - 3)
                pool.memset(qa[i][:, :, :, MROW:MROW + 2], 0.0)
                for n, (src, dst, places_1, places_2, place_3, ready) in enumerate((
                        (z[:, :, :], ka[i], slice(3, 6), slice(0, 2), 2, split_k_done),
                        (qv[:, :, 0, :], qa[i], slice(0, 5, 2), slice(1, 4, 2), 5, split_done))):
                    if n == 1 and i == 0:
                        hold(done["qv"], 2 * batches)
                    steps_before = 6 * X + 3 * n
                    whole = src.rearrange("p t (h d) -> p t h d", d=D)[:, :, HG * i:HG * i + HG, :]
                    parts = dst[:, :, :, 0:MROW].rearrange("p t h (a d) -> p (t h) a d", d=D)
                    part_1, left = stage[:, n, :, :, :], rest[:, n, :, :, :]
                    part_2 = parts[:, :, places_2, :]
                    pool.tensor_scalar(part_1, whole, 1.0, 0.0, ALU.mult, ALU.add).then_inc(split_q, 1)
                    hold(split_q, steps_before + 1)
                    pool.tensor_scalar(parts[:, :, places_1, :],
                                       part_1.rearrange("p t h (a d) -> p (t h) a d", a=1)
                                       .broadcast_to([P, TT * HG, 3, D]), 1.0, 0.0, ALU.mult, ALU.add)
                    pool.tensor_tensor(left, whole, part_1, ALU.subtract).then_inc(split_q, 1)
                    hold(split_q, steps_before + 2)
                    pool.tensor_scalar(part_2, left.rearrange("p t h (a d) -> p (t h) a d", a=1)
                                       .broadcast_to([P, TT * HG, 2, D]), 1.0, 0.0, ALU.mult, ALU.add)\
                        .then_inc(split_q, 1)
                    hold(split_q, steps_before + 3)
                    pool.tensor_tensor(parts[:, :, place_3, :], left.rearrange("p t h d -> p (t h) d"),
                                       part_2[:, :, 0, :], ALU.subtract).then_inc(ready, 1)

            def values(X, gx):
                i = gx % GB
                need(pool, dve_c, 2)
                need(pool, loaded, 16 * 5)
                hold(av_part, TT * (X - 3))
                for tt in range(TT):
                    ins = pool.tensor_tensor(
                        va[i][:, tt, :, 0:D],
                        qv[:, tt, 1, :].rearrange("p (h d) -> p h d", d=D)[:, HG * i:HG * i + HG, :],
                        bv_row[:, :].rearrange("p (h d) -> p h d", d=D)[:, HG * i:HG * i + HG, :], ALU.add)
                ins.then_inc(v_done, 1)

            def maxima(X, gx):
                i = gx % GB
                m = neg_max[gx % 2]
                hold(full["qT"], X + 1)
                hold(max_done, TT * HG * (X + 1))
                pool.tensor_scalar(qa[i][:, :, :, MROW:MROW + 1], m[:, :, :, :], 1.0, 0.0, ALU.mult, ALU.add)\
                    .then_inc(max_q, 1)
                hold(max_q, X + 1)
                pool.tensor_tensor(qa[i][:, :, :, MROW + 1:MROW + 2], m[:, :, :, :],
                                   qa[i][:, :, :, MROW:MROW + 1], ALU.subtract).then_inc(m_done, 1)

            def normalise(mv, ln, sem_q, i, out_of, src, ready):
                pool.tensor_scalar(ln[:, 0, :], mv[:, :, 1], 1.0, EPS, ALU.mult, ALU.add).then_inc(sem_q, 1)
                pool.tensor_scalar(ln[:, 2, :], mv[:, :, 0], -1.0, 0.0, ALU.mult, ALU.add).then_inc(sem_q, 1)
                hold(sem_q, 3 * i + 2)
                pool.tensor_tensor(ln[:, 1, :], ln[:, 0, :], neg_half[:, :], ALU.pow).then_inc(sem_q, 1)
                hold(sem_q, 3 * i + 3)
                for tt in range(TT):
                    pool.tensor_scalar(out_of(tt), src(tt), ln[:, 2, tt:tt + 1], ln[:, 1, tt:tt + 1],
                                       ALU.add, ALU.mult).then_inc(ready, 1)

            def dispatch(k, tiles):
                hold(route_done, k + 1)
                hold(blank_out, 16 * (1 + 2 * NB))
                for tt in tiles:
                    for c in range(2):
                        pool.indirect_dma_start(
                            out=rec_d, out_offset=bass.IndirectOffsetOnAxis(
                                ap=slot[:, c, tt, :].bitcast(U32), axis=0),
                            in_=rec[:, tt, c, :], in_offset=None, bounds_check=NE * CAP - 1,
                            oob_is_err=False).then_inc(rec_out, 16)

            def batch(b):
                for g in range(GB):
                    G = GB * b + g

                    def next_split(X, gx):
                        if live(X, NG):
                            hold(z_done, TT * (b + gx // GB + 1))
                            split(X, gx, b + gx // GB + 1)

                    def next_maxima():
                        if live(G + 1, NG):
                            maxima(G + 1, g + 1)

                    if g == 0:
                        if live(b - 2, NB):
                            dispatch(b - 2, (0,))
                        if live(b + 1, NB):
                            f = b + 1
                            hold(stat_a_done, f + 1)
                            hold(split_done, GB * f)
                            hold(full["zT"], f)
                            normalise(mv_a, ln_a, ln_q, f, lambda tt: z[:, tt, :], lambda tt: x_a[:, tt, :],
                                      z_done)
                            if isinstance(b, int) and b == -1:
                                router_constants()
                        if live(b - 2, NB):
                            dispatch(b - 2, (1,))
                        next_maxima()
                        if live(b - 2, NB):
                            dispatch(b - 2, (2, 3))
                    elif g == 1:
                        if live(b - 1, NB):
                            k = b - 1
                            hold(stat_b_done, b)
                            hold(rec_out, 16 * 2 * TT * k)
                            normalise(mv_b, ln_b, ln2_q, k,
                                      lambda tt: rec[:, tt, :, 0:C],
                                      lambda tt: x2[:, tt:tt + 1, :].broadcast_to([P, 2, C]), y_norm)
                            pool.tensor_scalar(rec[:, :, :, C + 1].bitcast(I32), dest[:, :, :], 1.0, 0.0,
                                               ALU.mult, ALU.add).then_inc(dest_q, 1)
                            hold(dest_q, 2 * k + 1)
                            pool.tensor_scalar(dest[:, :, :], dest[:, :, :], 1.0, float(T), ALU.mult, ALU.add)\
                                .then_inc(dest_q, 1)
                            hold(dest_q, 2 * k + 2)
                        next_maxima()
                        next_split(G + 3, g + 3)
                    elif g == 2:
                        next_split(G + 3, g + 3)
                        next_maxima()
                    else:
                        next_split(G + 3, g + 3)
                        next_maxima()
                        next_split(G + 4, g + 4)
                    if live(G + 3, NG):
                        values(G + 3, g + 3)
                    if g == 2 and live(b, NB):
                        hold(xb_in, 16 * (b + 1))
                        hold(done["out"], b)
                        pool.tensor_tensor(x_bo[:, :, :], x_b[:, :, :],
                                           bo_row[:, :].rearrange("p (a c) -> p a c", a=1).broadcast_to([P, TT, C]),
                                           ALU.add).then_inc(xbo_done, 1)

            run_batches(pool, batch)
            dispatch(NB - 1, range(TT))

            def scatter(e, r):
                for n in range(TT):
                    hold(y_done, TT * e + n + 1)
                    pool.indirect_dma_start(
                        out=y_d, out_offset=bass.IndirectOffsetOnAxis(
                            ap=meta[r][:, n, 1:2].bitcast(U32), axis=0),
                        in_=y[r][:, n, :], in_offset=None, bounds_check=2 * NTOK - 1,
                        oob_is_err=False).then_inc(y_out[r], 16)

            scatter(0, 0)
            scatter(1, 1)
            with pool.Fori(1, NE // 2) as i:
                scatter(2 * i, 0)
                scatter(2 * i + 1, 1)


_INS = ['L0_attn_x', 'L0_attn_w_att_val', 'L0_attn_wv_w', 'L0_attn_wv_b', 'L0_attn_out_w', 'L0_attn_out_b',
        'L0_ffn_rw1', 'L0_ffn_rb1', 'L0_ffn_rw2', 'L0_ffn_rb2', 'L0_ffn_ew1', 'L0_ffn_eb1', 'L0_ffn_ew2',
        'L0_ffn_eb2']
_OUTS = [((NB, T, C), 'float32')]


def kernel(**inputs):
    import numpy as _np
    import concourse.bacc as _bacc
    from concourse import mybir as _mybir
    from concourse.bass_utils import run_bass_kernel_spmd as _run

    nc = _bacc.Bacc("TRN2", target_bir_lowering=False, num_devices=1)
    arrays, args = {}, []
    for name in _INS:
        a = _np.ascontiguousarray(inputs[name])
        arrays[f"in_{name}_dram"] = a
        args.append(nc.dram_tensor(f"in_{name}_dram", a.shape, _mybir.dt.from_np(a.dtype), kind="ExternalInput").ap())
    for i, (shape, dtype) in enumerate(_OUTS):
        dt = _mybir.dt.from_np(_np.dtype(dtype))
        args.append(nc.dram_tensor(f"out_{i}_dram", shape, dt, kind="ExternalOutput").ap())
    build(nc, *args)
    r = _run(nc, [arrays], core_ids=[0])
    got = tuple(r.results[0][f"out_{i}_dram"] for i in range(len(_OUTS)))
    return got[0]
```
